# Optimizing a Trainium2 kernel written in Bass

```python
import numpy as np
import jax
import jax.numpy as jnp

def _softmax(x, axis=-1):
    return jax.nn.softmax(x, axis=axis)

def _gelu(x):
    return jax.nn.gelu(x, approximate=True)

def _silu(x):
    return jax.nn.silu(x)

def _sigmoid(x):
    return jax.nn.sigmoid(x)

def _layernorm(x, axis=-1, eps=1e-05):
    m = jnp.mean(x, axis=axis, keepdims=True)
    v = jnp.var(x, axis=axis, keepdims=True)
    return (x - m) / jnp.sqrt(v + eps)

def _scatter_add(tgt, idx, src, axis=0):
    return tgt.at[idx].add(src)

def _segment_sum(src, seg, n):
    return jax.ops.segment_sum(src, seg, n)
kernel_name = 'mk_seq_preln_d1_jaxref_r4_5b733f'

def setup_inputs(seed: int=0):
    np.random.seed(seed)
    _w = jnp.asarray

    def _L0_attn_setup():
        import jax, jax.numpy as jnp
        import numpy as np
        DIM = 256
        HEADS = 16
        HEAD_DIM = DIM // HEADS
        SCALE = float(HEAD_DIM ** (-0.25))
        ROPE_BASE = 10000.0

        def apply_rope(x):
            B, N, H, D = x.shape
            half = D // 2
            inv_freq = 1.0 / ROPE_BASE ** (jnp.arange(half, dtype=jnp.float32) / half)
            freqs = jnp.arange(N, dtype=jnp.float32)[:, None] * inv_freq[None, :]
            cos = jnp.cos(freqs)[None, :, None, :].astype(x.dtype)
            sin = jnp.sin(freqs)[None, :, None, :].astype(x.dtype)
            x1, x2 = (x[..., :half], x[..., half:])
            return jnp.concatenate([x1 * cos - x2 * sin, x1 * sin + x2 * cos], axis=-1)
        key = jax.random.key(seed)
        k1, k2, k3 = jax.random.split(key, 3)
        x = jax.random.normal(k1, (4, 1024, DIM), dtype=jnp.float32)
        w_qkv = jax.random.normal(k2, (DIM, 3 * DIM), dtype=jnp.float32) * 0.02
        w_out = jax.random.normal(k3, (DIM, DIM), dtype=jnp.float32) * 0.02
        return {'x': x, 'w_qkv': w_qkv, 'w_out': w_out}
    _L0_attn_in = _L0_attn_setup()

    def _L0_ffn_setup():
        import jax, jax.numpy as jnp
        import numpy as np
        import math
        GOLDEN_CENTER = 1.0 / math.e
        GOLDEN_LOWER = 0.5 - math.log(4.0 / 3.0)
        GOLDEN_UPPER = 0.5
        B, T, D = (4, 512, 256)
        E = 8
        I = 1024 // (E // 2)

        def _routing_weights(x, Wr, temperature):
            inh = jax.nn.sigmoid(x @ Wr / temperature)
            in_zone = (inh >= GOLDEN_LOWER) & (inh <= GOLDEN_UPPER)
            dist = jnp.abs(inh - GOLDEN_CENTER)
            w = jnp.exp(-dist / 0.1) * in_zone.astype(x.dtype)
            wsum = w.sum(axis=-1, keepdims=True)
            no_expert = wsum < 1e-08
            fb = jnp.exp(-dist / 0.3)
            _, top2 = jax.lax.top_k(fb, 2)
            fb_mask = jax.nn.one_hot(top2, E, dtype=x.dtype).sum(axis=-2)
            fb_w = fb * fb_mask
            fb_w = fb_w / jnp.clip(fb_w.sum(axis=-1, keepdims=True), 1e-08)
            w = jnp.where(no_expert, fb_w, w)
            wsum = w.sum(axis=-1, keepdims=True)
            return w / jnp.clip(wsum, 1e-08)
        key = jax.random.key(seed)
        k = jax.random.split(key, 6)
        s_d = 1.0 / math.sqrt(D)
        s_i = 1.0 / math.sqrt(I)
        return {'x': jax.random.normal(k[0], (B, T, D), jnp.float32), 'Wg': jax.random.normal(k[1], (E, D, I), jnp.float32) * s_d, 'Wu': jax.random.normal(k[2], (E, D, I), jnp.float32) * s_d, 'Wd': jax.random.normal(k[3], (E, I, D), jnp.float32) * s_i, 'Wr': jax.random.normal(k[4], (D, E), jnp.float32) * s_d, 'temperature': jnp.ones((1,), jnp.float32)}
    _L0_ffn_in = _L0_ffn_setup()
    _d = {'L0_attn_x': _L0_attn_in['x'], 'L0_attn_w_qkv': _L0_attn_in['w_qkv'], 'L0_attn_w_out': _L0_attn_in['w_out'], 'L0_ffn_Wg': _L0_ffn_in['Wg'], 'L0_ffn_Wu': _L0_ffn_in['Wu'], 'L0_ffn_Wd': _L0_ffn_in['Wd'], 'L0_ffn_Wr': _L0_ffn_in['Wr'], 'L0_ffn_temperature': _L0_ffn_in['temperature']}
    _x0 = _d['L0_attn_x']
    _d['L0_attn_x'] = jax.random.normal(jax.random.fold_in(jax.random.key(seed), 1), (1, 4096, 256), dtype=_x0.dtype)
    del _x0
    return _d

def reference(L0_attn_x, L0_attn_w_qkv, L0_attn_w_out, L0_ffn_Wg, L0_ffn_Wu, L0_ffn_Wd, L0_ffn_Wr, L0_ffn_temperature):

    def _L0_attn_ref(x, w_qkv, w_out):
        import jax, jax.numpy as jnp
        import numpy as np
        DIM = 256
        HEADS = 16
        HEAD_DIM = DIM // HEADS
        SCALE = float(HEAD_DIM ** (-0.25))
        ROPE_BASE = 10000.0

        def apply_rope(x):
            B, N, H, D = x.shape
            half = D // 2
            inv_freq = 1.0 / ROPE_BASE ** (jnp.arange(half, dtype=jnp.float32) / half)
            freqs = jnp.arange(N, dtype=jnp.float32)[:, None] * inv_freq[None, :]
            cos = jnp.cos(freqs)[None, :, None, :].astype(x.dtype)
            sin = jnp.sin(freqs)[None, :, None, :].astype(x.dtype)
            x1, x2 = (x[..., :half], x[..., half:])
            return jnp.concatenate([x1 * cos - x2 * sin, x1 * sin + x2 * cos], axis=-1)
        B, N, D = x.shape
        qkv = x @ w_qkv
        q, k, v = jnp.split(qkv, 3, axis=-1)
        q = q.reshape(B, N, HEADS, HEAD_DIM)
        k = k.reshape(B, N, HEADS, HEAD_DIM)
        v = v.reshape(B, N, HEADS, HEAD_DIM)
        q = apply_rope(q)
        k = apply_rope(k)
        q = jax.nn.elu(q * SCALE) + 1.0
        k = jax.nn.elu(k * SCALE) + 1.0
        qT = jnp.moveaxis(q, 1, 0)
        kT = jnp.moveaxis(k, 1, 0)
        vT = jnp.moveaxis(v, 1, 0)
        kv0 = jnp.zeros((B, HEADS, HEAD_DIM, HEAD_DIM), dtype=q.dtype)
        ks0 = jnp.zeros((B, HEADS, HEAD_DIM), dtype=q.dtype)

        def step(carry, qkv_t):
            kv, ks = carry
            qt, kt, vt = qkv_t
            kv = kv + jnp.einsum('bhd,bhm->bhdm', kt, vt)
            ks = ks + kt
            denom = jnp.maximum(jnp.einsum('bhd,bhd->bh', qt, ks), 1e-06)
            out_t = jnp.einsum('bhd,bhdm->bhm', qt, kv) / denom[..., None]
            return ((kv, ks), out_t)
        _, outT = jax.lax.scan(step, (kv0, ks0), (qT, kT, vT))
        out = jnp.moveaxis(outT, 0, 1).reshape(B, N, D)
        return out @ w_out

    def _L0_ffn_ref(x, Wg, Wu, Wd, Wr, temperature):
        import jax, jax.numpy as jnp
        import numpy as np
        import math
        GOLDEN_CENTER = 1.0 / math.e
        GOLDEN_LOWER = 0.5 - math.log(4.0 / 3.0)
        GOLDEN_UPPER = 0.5
        B, T, D = (4, 512, 256)
        E = 8
        I = 1024 // (E // 2)

        def _routing_weights(x, Wr, temperature):
            inh = jax.nn.sigmoid(x @ Wr / temperature)
            in_zone = (inh >= GOLDEN_LOWER) & (inh <= GOLDEN_UPPER)
            dist = jnp.abs(inh - GOLDEN_CENTER)
            w = jnp.exp(-dist / 0.1) * in_zone.astype(x.dtype)
            wsum = w.sum(axis=-1, keepdims=True)
            no_expert = wsum < 1e-08
            fb = jnp.exp(-dist / 0.3)
            _, top2 = jax.lax.top_k(fb, 2)
            fb_mask = jax.nn.one_hot(top2, E, dtype=x.dtype).sum(axis=-2)
            fb_w = fb * fb_mask
            fb_w = fb_w / jnp.clip(fb_w.sum(axis=-1, keepdims=True), 1e-08)
            w = jnp.where(no_expert, fb_w, w)
            wsum = w.sum(axis=-1, keepdims=True)
            return w / jnp.clip(wsum, 1e-08)
        weights = _routing_weights(x, Wr, temperature)
        gate = jnp.einsum('btd,edi->beti', x, Wg)
        up = jnp.einsum('btd,edi->beti', x, Wu)
        h = jax.nn.silu(gate) * up
        e_out = jnp.einsum('beti,eid->betd', h, Wd)
        out = jnp.einsum('bte,betd->btd', weights, e_out)
        return out
    x = L0_attn_x
    x = x + _L0_attn_ref(_layernorm(x, axis=-1), L0_attn_w_qkv, L0_attn_w_out)
    x = x + _L0_ffn_ref(_layernorm(x, axis=-1), L0_ffn_Wg, L0_ffn_Wu, L0_ffn_Wd, L0_ffn_Wr, L0_ffn_temperature)
    return x

_drawn_inputs = setup_inputs


def setup_inputs(seed=0):
    import zlib

    import numpy as np

    out = dict(_drawn_inputs(seed))
    spreads = {}
    factors = {'L0_attn_w_qkv': 4.416, 'L0_attn_w_out': 4.371}
    for name, (base, spread) in spreads.items():
        noise = np.random.default_rng([zlib.crc32(name.encode()), seed]).standard_normal(out[name].shape)
        drawn = base * np.exp(spread * noise) if base else spread * noise
        out[name] = jnp.asarray(drawn.astype(out[name].dtype))
    for name, factor in factors.items():
        out[name] = (out[name] * factor).astype(out[name].dtype)
    return out
```

```python
from contextlib import ExitStack

import numpy as np

import concourse.bass as bass
from concourse import mybir

F32 = mybir.dt.float32
F32R = mybir.dt.float32r
F16 = mybir.dt.float16
BF16 = mybir.dt.bfloat16
ALU = mybir.AluOpType
ACT = mybir.ActivationFunctionType
AX = mybir.AxisListType

P = 128
N, D = 4096, 256
B = 512
NB = N // B
NT = B // P
KD = D // P
H, HD = 16, 16
HALF = HD // 2
NP = H // 2
E, I = 8, 256
KI = I // P
UNITS = E * KI
W1 = HD + 1
WV = 3 * W1
SCALE = float(HD ** -0.25)
EPS = 1e-5
ASCALE = 1.0 / 16.0
G_CENTER = 1.0 / float(np.e)
G_LOWER = 0.5 - float(np.log(4.0 / 3.0))
G_UPPER = 0.5
SLOTS = 3 * UNITS
NWB = 3


class Part:

    def __init__(self, name, sems):
        self.name, self.sems = name, sems
        self.ops = {e: [] for e in ENGINES}
        self.number = {}
        self.count = {e: 0 for e in ENGINES}

    def add(self, engine, slot, event, fn, *waits):
        self.ops[engine].append((slot, event, fn, waits))

    def close(self):
        for engine, ops in self.ops.items():
            ops.sort(key=lambda op: op[0])
            for _, event, _, _ in ops:
                if event is not None and engine != "sync":
                    self.count[engine] += 1
                    self.number[engine, event] = self.count[engine]


ENGINES = ("tensor", "scalar", "vector", "gpsimd", "sync")


def bcast(ap, axis, n):
    ap = ap.unsqueeze(axis)
    shape = list(ap.shape)
    shape[axis] = n
    return ap.broadcast_to(shape)


def build(nc, x, xT, w_qkv, w_out, Wg, Wu, Wd, Wr, temperature, tab, outT, w_scr, x1_scr):
    ctx = ExitStack()

    def sb(name, shape, dt=F32):
        return ctx.enter_context(nc.sbuf_tensor(name, shape, dt))

    def sem(name):
        return ctx.enter_context(nc.semaphore(name))

    with ctx:
        ident = sb("ident", [P, P])
        ident16 = sb("ident16", [P, P], F16)
        cmask = sb("cmask", [P, P])
        mean_w = sb("mean_w", [P, P])
        iota = sb("iota", [P, E])
        iota_i = sb("iota_i", [P, E], mybir.dt.int32)
        temp = sb("temp", [P, 1])
        rtemp = sb("rtemp", [P, 1])
        mhalf = sb("mhalf", [P, NT])
        wqkv_p = [sb(f"wqkv_{s}", [P, KD, 3 * D], F32R) for s in ("hi", "lo")]
        wout_p = [sb(f"wout_{s}", [P, KD, D], F32R) for s in ("hi", "lo")]
        wg_p = [sb(f"wg_{s}", [P, E, KD, I], F32R) for s in ("hi", "lo")]
        wu_p = [sb(f"wu_{s}", [P, E, KD, I], F32R) for s in ("hi", "lo")]
        wd_p = [sb(f"wd_{s}", [P, E, KI, D], F32R) for s in ("hi", "lo")]
        wr_sb = sb("wr_sb", [P, KD, E])
        xraw = sb("xraw", [P, KD, B])
        xnat = sb("xnat", [P, 2, D])
        tabs = sb("tabs", [P, NT, 3 * HALF])
        xo = [sb(f"xo_{s}", [P, KD, B], F32R) for s in ("hi", "lo")]
        bst = sb("bst", [P, 6])
        idle = sb("idle", [P, 1])
        ve = sb("ve", [P, NT])
        v2n = sb("v2n", [P, NT])
        r2n = sb("r2n", [P, NT])
        mv = sb("mv", [P, NT, 2])
        rstd1 = sb("rstd1", [P, NT])
        qk = sb("qk", [P, 2 * D])
        rop = sb("rop", [P, 2 * D])
        rop2 = sb("rop2", [P, 2 * D])
        ex = sb("ex", [P, 2 * D])
        vs = sb("vs", [P, D])
        stack = sb("stack", [P, 2 * H, 4, HD], F16)
        kT = sb("kT", [P, NP, P], F16)
        qbd = sb("qbd", [P, NP, 2, P], F16)
        vx = sb("vx", [P, H, 3, W1], BF16)
        am = sb("am", [P, 2, 4 * P])
        a_p = [sb(f"a_{s}", [P, H, P], F16) for s in ("hi", "lo")]
        osb = sb("osb", [P, H, W1])
        den = sb("den", [P, H])
        rec = sb("rec", [P, H])
        onrm = sb("onrm", [P, D])
        st_d = sb("st_d", [P, NP, W1])
        st_s = sb("st_s", [P, NP, W1])
        st_r = sb("st_r", [P, NP, W1])
        st_x = sb("st_x", [P, NP, 3, W1], BF16)
        x1 = sb("x1", [P, KD, B])
        sq = sb("sq", [P, B])
        rt = sb("rt", [P, B])
        R = {n: sb(f"r_{n}", [P, NT, E]) for n in
             ("z", "th", "inh", "zone", "zone2", "dist", "e1", "fb", "w0", "eq", "c", "s1", "nd", "s2", "fw", "w", "wo")}
        R1 = {n: sb(f"q_{n}", [P, NT]) for n in ("ws", "no", "yes", "m", "ix", "m2", "ix2", "fs", "w2")}
        x2 = [sb(f"x2_{s}", [P, KD, B], F32R) for s in ("hi", "lo")]
        x1r = sb("x1r", [P, KD, B])
        wb = sb("wb", [P, NWB, B])
        hb = sb("hb", [P, 2, B])
        h_p = [sb(f"h_{s}", [P, 2, B], F32R) for s in ("hi", "lo")]
        G, U, Y0, Y1, R0, R1b, R2, R3 = (
            ctx.enter_context(nc.psum_tensor(n, [P, 512], F32))
            for n in ("gate", "up", "y0", "y1", "front0", "front1", "back0", "back1"))
        Y, FR, BK = [Y0, Y1], [R0, R1b], [R2, R3]

        sems = {(p, e): sem(f"{p}_{e}") for p in ("setup", "att", "moe") for e in ENGINES[:4]}
        dma_names = ("c_temp", "c_wr", "c_wqkv", "c_wout", "x_raw", "x_nat0", "x_nat1", "tab", "x1_out", "w_out",
                     "x1_in", "y_out") + tuple(f"wb{i}" for i in range(NWB)) + tuple(f"slab{i}" for i in range(NWB))
        carrier = sem("carrier")
        dsem = {n: sem(f"dma_{n}") for n in dma_names}

        setup, att, moe = (Part(n, sems) for n in ("setup", "att", "moe"))
        parts = {"setup": setup, "att": att, "moe": moe}

        def at(part, engine, *event):
            return (part, engine, event, 0)

        def before(part, engine, *event):
            return (part, engine, event, 1)

        def dma(name, per_block, k, back=0):
            return ("dma", name, (per_block, k), back)

        def S(engine, *event):
            return at("setup", engine, *event)

        add = setup.add
        wq_raw = wb[:, :, :].rearrange("p a b -> p (a b)").rearrange("p (k n) -> p k n", k=KD)
        wo_raw = x1r[:, 0, :].rearrange("p (k n) -> p k n", k=KD)
        add("sync", 0, None, lambda e, b: e.dma_start(wq_raw, w_qkv.rearrange("(k p) n -> p k n", p=P))
            .then_inc(dsem["c_wqkv"], 16))
        add("sync", 0, None, lambda e, b: e.dma_start(wo_raw, w_out.rearrange("(k p) n -> p k n", p=P))
            .then_inc(dsem["c_wout"], 16))
        add("sync", 0, None, lambda e, b: e.dma_start(wr_sb[:, :, :], Wr.rearrange("(k p) n -> p k n", p=P))
            .then_inc(dsem["c_wr"], 16))
        add("sync", 0, None, lambda e, b: e.dma_start(temp[:, :], temperature.rearrange("(a n) -> a n", a=1)
                                                      .broadcast_to([P, 1])).then_inc(dsem["c_temp"], 16))
        add("vector", 0, ("ones",), lambda e, b: e.memset(mean_w[:, :], 1.0 / D))
        add("vector", 0, ("mhalf",), lambda e, b: e.memset(mhalf[:, :], -0.5))
        add("vector", 0, ("rtemp",), lambda e, b: e.reciprocal(rtemp[:, :], temp[:, :]), ("once", "c_temp", 1, 0))
        add("gpsimd", 0, ("id0",), lambda e, b: e.memset(ident[:, :], 0.0))
        add("gpsimd", 0, ("mask0",), lambda e, b: e.memset(cmask[:, :], ASCALE))
        add("gpsimd", 0, ("id",), lambda e, b: e.affine_select(
            out=ident[:, :], in_=ident[:, :], compare_op=ALU.not_equal, fill=1.0, base=0,
            pattern=[[-1, P]], channel_multiplier=1), S("gpsimd", "id0"))
        add("gpsimd", 0, ("mask",), lambda e, b: e.affine_select(
            out=cmask[:, :], in_=cmask[:, :], compare_op=ALU.is_ge, fill=0.0, base=0,
            pattern=[[1, P]], channel_multiplier=-1), S("gpsimd", "mask0"))
        add("gpsimd", 0, ("iota_i",), lambda e, b: e.iota(iota_i[:, :], pattern=[[1, E]], base=0, channel_multiplier=0))
        add("vector", 0, ("iota",), lambda e, b: e.tensor_copy(iota[:, :], iota_i[:, :]), S("gpsimd", "iota_i"))
        add("vector", 0, ("id16",), lambda e, b: e.tensor_copy(ident16[:, :], ident[:, :]), S("gpsimd", "id"))
        add("vector", 0, ("z_qbd",), lambda e, b: e.memset(qbd[:, :, :, :].rearrange("p a b c -> p (a b c)"), 0.0))
        add("vector", 0, ("z_vx",), lambda e, b: e.memset(vx[:, :, :, :].rearrange("p a b c -> p (a b c)"), 0.0))
        add("vector", 0, ("one_vx",), lambda e, b: e.memset(vx[:, :, 0, HD], 1.0), S("vector", "z_vx"))
        add("vector", 0, ("z_sx",), lambda e, b: e.memset(st_x[:, :, :, :].rearrange("p a b c -> p (a b c)"), 0.0))
        add("vector", 0, ("z_rt",), lambda e, b: e.memset(rt[:, :], 0.0))
        add("vector", 0, ("z_ss",), lambda e, b: e.memset(st_s[:, :, :].rearrange("p a b -> p (a b)"), 0.0))

        def col_means(e, b):
            for k in range(KD):
                e.matmul(R0[:, :], mean_w[:, :], wq_raw[:, k, 0:2 * D], start=(k == 0), stop=(k == KD - 1))
            for k in range(KD):
                m = e.matmul(R1b[:, 0:D], mean_w[:, :], wq_raw[:, k, 2 * D:], start=(k == 0), stop=(k == KD - 1))
            return m
        add("tensor", 0, ("colmean",), col_means, S("vector", "ones"), ("once", "c_wqkv", 1, 0))
        for k in range(KD):
            add("vector", 1, ("wc", k, 0), lambda e, b, k=k: e.tensor_tensor(
                wq_raw[:, k, 0:2 * D], wq_raw[:, k, 0:2 * D], R0[:, :], ALU.subtract), S("tensor", "colmean"))
            add("vector", 1, ("wc", k, 1), lambda e, b, k=k: e.tensor_tensor(
                wq_raw[:, k, 2 * D:], wq_raw[:, k, 2 * D:], R1b[:, 0:D], ALU.subtract), S("tensor", "colmean"))
            add("scalar", 1, ("wqkv_hi", k), lambda e, b, k=k: e.activation(
                wqkv_p[0][:, k, :], wq_raw[:, k, :], ACT.Copy), S("vector", "wc", k, 0), S("vector", "wc", k, 1))
            add("vector", 2, ("wqkv_lo", k), lambda e, b, k=k: e.tensor_tensor(
                wqkv_p[1][:, k, :], wq_raw[:, k, :], wqkv_p[0][:, k, :].bitcast(F32), ALU.subtract),
                S("scalar", "wqkv_hi", k))
        add("scalar", 1, ("wout_hi",), lambda e, b: e.activation(wout_p[0][:, :, :], wo_raw, ACT.Copy),
            ("once", "c_wout", 1, 0))
        add("vector", 2, ("wout_lo",), lambda e, b: e.tensor_tensor(
            wout_p[1][:, :, :], wo_raw, wout_p[0][:, :, :].bitcast(F32), ALU.subtract), S("scalar", "wout_hi"))

        slabs = [(src, dst, ex_) for ex_ in range(E) for src, dst in ((Wg, wg_p), (Wu, wu_p), (Wd, wd_p))]
        for n, (src, dst, ex_) in enumerate(slabs):
            s, slot = n % NWB, 2 + 2 * n
            free = [S("vector", "wqkv_lo", k) for k in range(KD)] + [S("scalar", "wqkv_hi", k) for k in range(KD)]
            if n >= NWB:
                free = [S("gpsimd" if (n - NWB) % 2 else "vector", "slab_lo", n - NWB), S("scalar", "slab_hi", n - NWB)]
            raw = wb[:, s, :].rearrange("p (k n) -> p k n", k=KD)
            add("sync", slot, None, lambda e, b, raw=raw, src=src, ex_=ex_, s=s: e.dma_start(
                raw, src[ex_].rearrange("(k p) n -> p k n", p=P)).then_inc(dsem[f"slab{s}"], 16), *free)
            add("scalar", slot, ("slab_hi", n), lambda e, b, raw=raw, dst=dst, ex_=ex_: e.activation(
                dst[0][:, ex_, :, :], raw, ACT.Copy), ("once", f"slab{s}", n // NWB + 1, 0))
            add("gpsimd" if n % 2 else "vector", slot, ("slab_lo", n), lambda e, b, raw=raw, dst=dst, ex_=ex_: e.tensor_tensor(
                dst[1][:, ex_, :, :], raw, dst[0][:, ex_, :, :].bitcast(F32), ALU.subtract),
                S("scalar", "slab_hi", n))
        last_slabs = [S("gpsimd" if n % 2 else "vector", "slab_lo", n) for n in range(len(slabs) - 2, len(slabs))]

        def A(engine, *event):
            return at("att", engine, *event)

        def Ab(engine, *event):
            return before("att", engine, *event)

        def M(engine, *event):
            return at("moe", engine, *event)

        def Mb(engine, *event):
            return before("moe", engine, *event)

        add = att.add

        add("sync", 0, None, lambda e, b: e.dma_start(
            xraw[:, :, :], xT[:, bass.ds(b, B)].rearrange("(k p) n -> p k n", p=P)).then_inc(dsem["x_raw"], 16),
            Ab("vector", "x1", KD - 1))
        add("sync", 0, None, lambda e, b: e.dma_start(
            tabs[:, :, :], tab[bass.ds(b, B), :].rearrange("(t p) n -> p t n", p=P)).then_inc(dsem["tab"], 16),
            Ab("vector", "cos", NT - 1), Ab("gpsimd", "sin2", NT - 1))

        for k in range(KD):
            add("scalar", 1, ("x_hi", k), lambda e, b, k=k: e.activation(xo[0][:, k, :], xraw[:, k, :], ACT.Copy),
                dma("x_raw", 1, 1), Ab("tensor", "proj"))
            add("vector", 1, ("x_lo", k), lambda e, b, k=k: e.tensor_tensor(
                xo[1][:, k, :], xraw[:, k, :], xo[0][:, k, :].bitcast(F32), ALU.subtract), A("scalar", "x_hi", k))

        for t in range(NT):
            f = 2 + 8 * t
            tok = slice(t * P, (t + 1) * P)
            s = t % 2
            add("sync", max(0, f - 6), None, lambda e, b, t=t, s=s: e.dma_start(
                xnat[:, s, :], x[bass.ds(b + t * P, P), :]).then_inc(dsem[f"x_nat{s}"], 16),
                (A if t >= 2 else Ab)("vector", "bn", t - 2 if t >= 2 else t + 2))
            add("vector", max(0, f - 2), ("bn", t), lambda e, b, s=s: e.bn_stats(bst[:, :], xnat[:, s, :]),
                dma(f"x_nat{s}", 2, t // 2 + 1), (A if t else Ab)("vector", "mv", t - 1 if t else NT - 1))
            add("vector", max(0, f - 2), ("mv", t), lambda e, b, t=t: (e.memset(idle[:, :], 0.0), e.bn_aggr(mv[:, t, :], bst[:, :]))[-1],
                A("vector", "bn", t), Ab("gpsimd", "rstd1", t))
            add("vector", max(0, f - 2), ("ve", t), lambda e, b, t=t: e.tensor_scalar(
                ve[:, t:t + 1], mv[:, t, 1:2], EPS, None, ALU.add), A("vector", "mv", t))
            add("gpsimd", max(0, f - 2), ("rstd1", t), lambda e, b, t=t: e.tensor_tensor(
                rstd1[:, t:t + 1], ve[:, t:t + 1], mhalf[:, 0:1], ALU.pow),
                A("vector", "ve", t), Ab("scalar", "v", t), S("vector", "mhalf"))

            def qkv(e, b, tok=tok):
                n = 0
                for k in range(KD):
                    for xi, wis in ((0, (0, 1)), (1, (0,))):
                        for wi in wis:
                            lhs = xo[xi][:, k, tok]
                            first, last = n == 0, n == 3 * KD - 1
                            e.matmul(R0[:, :], lhs, wqkv_p[wi][:, k, 0:2 * D], start=first, stop=last)
                            m = e.matmul(R1b[:, 0:D], lhs, wqkv_p[wi][:, k, 2 * D:], start=first, stop=last)
                            n += 1
                return m
            prev_t = (lambda eng, *ev: A(eng, *ev, t - 1)) if t else (lambda eng, *ev: Ab(eng, *ev, NT - 1))
            add("tensor", f, ("qkv", t), qkv, A("scalar", "x_hi", KD - 1), A("vector", "x_lo", KD - 1),
                prev_t("vector", "kT"), prev_t("vector", "qT1"), prev_t("scalar", "qT0"),
                S("vector", "wqkv_lo", KD - 1))

            add("scalar", f + 1, ("qk", t), lambda e, b, t=t: e.activation(
                qk[:, :], R0[:, :], ACT.Copy, scale=rstd1[:, t:t + 1]),
                A("tensor", "qkv", t), A("gpsimd", "rstd1", t), prev_t("vector", "q_lo"), prev_t("gpsimd", "k_lo"))
            add("scalar", f + 1, ("v", t), lambda e, b, t=t: e.activation(
                vs[:, :], R1b[:, 0:D], ACT.Copy, scale=rstd1[:, t:t + 1]), prev_t("gpsimd", "v3"))

            qk_h = qk[:, :].rearrange("p (h s d) -> p h s d", s=2, d=HALF)
            r2_h = rop2[:, :].rearrange("p (h s d) -> p h s d", s=2, d=HALF)
            add("vector", f + 1, ("cos", t), lambda e, b, t=t: e.tensor_tensor(
                rop[:, :].rearrange("p (h d) -> p h d", d=HALF), qk[:, :].rearrange("p (h d) -> p h d", d=HALF),
                bcast(tabs[:, t, 0:HALF], 1, 4 * H), ALU.mult),
                A("scalar", "qk", t), dma("tab", 1, 1), prev_t("scalar", "relu"), prev_t("scalar", "exp"))
            for s2, at_ in ((0, HALF), (1, 2 * HALF)):
                add("gpsimd", f + 1, ("sin" + str(s2 + 1), t), lambda e, b, t=t, s2=s2, at_=at_: e.tensor_tensor(
                    r2_h[:, :, s2, :], qk_h[:, :, 1 - s2, :], bcast(tabs[:, t, at_:at_ + HALF], 1, 2 * H), ALU.mult),
                    A("scalar", "qk", t), dma("tab", 1, 1), prev_t("vector", "phi"))
            add("vector", f + 2, ("rope", t), lambda e, b: e.tensor_tensor(rop[:, :], rop[:, :], rop2[:, :], ALU.add),
                A("vector", "cos", t), A("gpsimd", "sin1", t), A("gpsimd", "sin2", t))
            add("scalar", f + 2, ("exp", t), lambda e, b: e.activation(ex[:, :], rop[:, :], ACT.Exp),
                A("vector", "rope", t), prev_t("vector", "phi"))
            add("scalar", f + 2, ("relu", t), lambda e, b: e.activation(rop2[:, :], rop[:, :], ACT.Relu),
                A("vector", "rope", t))
            add("vector", f + 3, ("phi", t), lambda e, b: e.scalar_tensor_tensor(
                out=qk[:, :], in0=ex[:, :], scalar=1.0, in1=rop2[:, :], op0=ALU.min, op1=ALU.add),
                A("scalar", "exp", t), A("scalar", "relu", t), A("gpsimd", "sin2", t), A("vector", "cos", t))
            f_q = bcast(qk[:, 0:D].rearrange("p (h d) -> p h d", d=HD), 2, 2)
            f_k = bcast(qk[:, D:].rearrange("p (h d) -> p h d", d=HD), 2, 2)
            add("scalar", f + 3, ("q_hi", t), lambda e, b, f_q=f_q: e.activation(stack[:, 0:H, 0:2, :], f_q, ACT.Copy),
                A("vector", "phi", t), prev_t("tensor", "state"))
            add("scalar", f + 3, ("k_hi", t), lambda e, b, f_k=f_k: e.activation(stack[:, H:, 0::2, :], f_k, ACT.Copy))
            add("vector", f + 3, ("q_lo", t), lambda e, b, f_q=f_q: e.tensor_tensor(
                stack[:, 0:H, 2:4, :], f_q, stack[:, 0:H, 0:2, :], ALU.subtract), A("scalar", "q_hi", t))
            add("gpsimd", f + 3, ("k_lo", t), lambda e, b, f_k=f_k: e.tensor_tensor(
                stack[:, H:, 1::2, :], f_k, stack[:, H:, 0::2, :], ALU.subtract), A("scalar", "k_hi", t))
            v_h = vs[:, :].rearrange("p (h d) -> p h d", d=HD)
            add("scalar", f + 3, ("v1", t), lambda e, b: e.activation(vx[:, :, 0, 0:HD], v_h, ACT.Copy),
                A("scalar", "v", t), prev_t("tensor", "state"), S("vector", "z_ss"))
            add("gpsimd", f + 3, ("vr", t), lambda e, b: e.tensor_tensor(v_h, v_h, vx[:, :, 0, 0:HD], ALU.subtract),
                A("scalar", "v1", t))
            add("scalar", f + 4, ("v2", t), lambda e, b: e.activation(vx[:, :, 1, 0:HD], v_h, ACT.Copy),
                A("gpsimd", "vr", t))
            add("gpsimd", f + 4, ("v3", t), lambda e, b: e.tensor_tensor(
                vx[:, :, 2, 0:HD], v_h, vx[:, :, 1, 0:HD], ALU.subtract), A("scalar", "v2", t))

            kTp, qTp = (r[:, :].bitcast(F16).rearrange("p (a b) -> p a b", a=NP) for r in (R0, R1b))

            def turn(e, b, dst, first):
                for p in range(NP):
                    m = e.transpose(dst[:, p, :], stack[:, first + 2 * p:first + 2 * p + 2, :, :]
                                    .rearrange("p h c d -> p (h c d)"), ident16[:, :])
                return m
            add("tensor", f + 4, ("k_T", t), lambda e, b, d=kTp: turn(e, b, d, H),
                A("scalar", "k_hi", t), A("gpsimd", "k_lo", t), A("scalar", "qk", t), S("vector", "id16"))
            add("tensor", f + 4, ("q_T", t), lambda e, b, d=qTp: turn(e, b, d, 0),
                A("scalar", "q_hi", t), A("vector", "q_lo", t), A("scalar", "v", t))
            add("vector", f + 4, ("kT", t), lambda e, b, s_=kTp: e.tensor_copy(kT[:, :, :], s_),
                A("tensor", "k_T", t), prev_t("tensor", "qk3"))
            add("scalar", f + 4, ("qT0", t), lambda e, b, s_=qTp: e.activation(qbd[0:64, :, 0, :], s_[0:64], ACT.Copy),
                A("tensor", "q_T", t), prev_t("tensor", "av1"), S("vector", "z_qbd"))
            add("vector", f + 4, ("qT1", t), lambda e, b, s_=qTp: e.tensor_copy(qbd[64:P, :, 1, :], s_[64:P]),
                A("tensor", "q_T", t), prev_t("tensor", "av1"))

            for r in range(4):
                bank, g = BK[r % 2], f + 5 + r // 2
                if r >= 2:
                    free = (A("vector", f"mask{r - 2}", t),)
                elif t:
                    free = (A("vector", "st1", t - 1), A("vector", "o_lo", t - 1))
                else:
                    free = (Ab("scalar", "wt"), Ab("vector", "z"))
                add("tensor", g, (f"qk{r}", t), lambda e, b, r=r, bank=bank: [e.matmul(
                    bank[:, 2 * P * j:2 * P * (j + 1)], kT[:, 2 * r + j, :],
                    qbd[:, 2 * r + j, :, :].rearrange("p a b -> p (a b)"), start=True, stop=True)
                    for j in range(2)][-1],
                    A("vector", "kT", t), A("vector", "qT1", t), A("scalar", "qT0", t), *free)
                add("vector", g, (f"mask{r}", t), lambda e, b, r=r, bank=bank: e.tensor_tensor(
                    am[:, r % 2, :].rearrange("p (h n) -> p h n", h=4), bank[:, :].rearrange("p (h n) -> p h n", h=4),
                    bcast(cmask[:, :], 1, 4), ALU.mult),
                    A("tensor", f"qk{r}", t), S("gpsimd", "mask"),
                    A("gpsimd", f"a_lo{r - 2}", t) if r >= 2 else prev_t("gpsimd", f"a_lo{r + 2}"))
                a4 = am[:, r % 2, :].rearrange("p (h n) -> p h n", h=4)
                add("scalar", g, (f"a_hi{r}", t), lambda e, b, r=r, a4=a4: e.activation(
                    a_p[0][:, 4 * r:4 * r + 4, :], a4, ACT.Copy),
                    A("vector", f"mask{r}", t), prev_t("tensor", "av1"))
                add("gpsimd", g, (f"a_lo{r}", t), lambda e, b, r=r, a4=a4: e.tensor_tensor(
                    a_p[1][:, 4 * r:4 * r + 4, :], a4, a_p[0][:, 4 * r:4 * r + 4, :], ALU.subtract),
                    A("scalar", f"a_hi{r}", t))

            def attend(e, b, g):
                for h in range(8 * g, 8 * g + 8):
                    o = BK[g][:, (h % 8) * WV:(h % 8 + 1) * WV]
                    e.matmul(o, qbd[:, h // 2, h % 2, :], st_x[:, h // 2, :, :].rearrange("p a b -> p (a b)"),
                             start=(h % 8 == 0), stop=False, skip_group_check=True)
                for h in range(8 * g, 8 * g + 8):
                    o = BK[g][:, (h % 8) * WV:(h % 8 + 1) * WV]
                    for a in a_p:
                        m = e.matmul(o, a[:, h, :], vx[:, h, :, :].rearrange("p a b -> p (a b)"),
                                     start=False, stop=(h % 8 == 7), skip_group_check=True)
                return m
            for g in range(2):
                add("tensor", f + 8 + g, (f"av{g}", t), lambda e, b, g=g: attend(e, b, g),
                    A("vector", f"mask{2 + g}", t), A("gpsimd", f"a_lo{2 * g + 1}", t), A("scalar", f"a_hi{2 * g + 1}", t),
                    A("gpsimd", "v3", t), A("scalar", "v2", t),
                    *((prev_t("gpsimd", "s3"), prev_t("scalar", "s2"))), S("vector", "z_ss"))
                add("vector", f + 8 + g, (f"o{g}", t), lambda e, b, g=g: e.tensor_reduce(
                    osb[:, 8 * g:8 * g + 8, :],
                    BK[g][:, 0:8 * WV].rearrange("p (h s d) -> p h d s", s=3, d=W1), AX.X, ALU.add),
                    A("tensor", f"av{g}", t), prev_t("vector", "norm"))

            def state(e, b):
                for p in range(NP):
                    m = e.matmul(BK[p // 4][:, (p % 4) * 2 * WV:(p % 4 + 1) * 2 * WV],
                                 stack[:, H + 2 * p:H + 2 * p + 2, :, :].rearrange("p h c d -> p (h c d)"),
                                 vx[:, 2 * p:2 * p + 2, :, :].rearrange("p h a b -> p (h a b)"),
                                 start=(p % 4 == 0), stop=(p % 4 == 3), skip_group_check=True)
                return m
            add("tensor", f + 10, ("state", t), state, A("vector", "o0", t), A("vector", "o1", t))
            for g in range(2):
                for hh in range(2):
                    rows = slice(64 * hh, 64 * hh + 64)
                    add("vector", f + 10, (f"st{g}_{hh}" if (g, hh) != (1, 1) else "st1", t),
                        lambda e, b, g=g, hh=hh, rows=rows: e.tensor_reduce(
                            st_d[rows, 4 * g:4 * g + 4, :],
                            BK[g][rows, 0:8 * WV].rearrange("p (q h s d) -> p q h d s", h=2, s=3, d=W1)[:, :, hh, :, :],
                            AX.X, ALU.add), A("tensor", "state", t), prev_t("vector", "ss"))
            add("vector", f + 11, ("ss", t), lambda e, b: e.scalar_tensor_tensor(
                out=st_s[:, :, :], in0=st_d[:, :, :], scalar=ASCALE, in1=st_s[:, :, :], op0=ALU.mult, op1=ALU.add),
                A("vector", "st1", t), A("vector", "st0_0", t), A("vector", "st0_1", t), A("vector", "st1_0", t),
                prev_t("gpsimd", "sr"), prev_t("scalar", "s1"), S("vector", "z_ss"))
            add("scalar", f + 11, ("s1", t), lambda e, b: e.activation(st_x[:, :, 0, :], st_s[:, :, :], ACT.Copy),
                A("vector", "ss", t), A("tensor", "av1", t), S("vector", "z_sx"))
            add("gpsimd", f + 11, ("sr", t), lambda e, b: e.tensor_tensor(
                st_r[:, :, :], st_s[:, :, :], st_x[:, :, 0, :], ALU.subtract), A("scalar", "s1", t),
                prev_t("gpsimd", "s3"))
            add("scalar", f + 11, ("s2", t), lambda e, b: e.activation(st_x[:, :, 1, :], st_r[:, :, :], ACT.Copy),
                A("gpsimd", "sr", t))
            add("gpsimd", f + 11, ("s3", t), lambda e, b: e.tensor_tensor(
                st_x[:, :, 2, :], st_r[:, :, :], st_x[:, :, 1, :], ALU.subtract), A("scalar", "s2", t))

            add("vector", f + 10, ("den", t), lambda e, b: e.tensor_scalar(
                den[:, :], osb[:, :, HD], 1.0 / ASCALE, 1e-6, ALU.mult, ALU.max),
                A("vector", "o0", t), A("vector", "o1", t), prev_t("vector", "rec"))
            add("vector", f + 10, ("rec", t), lambda e, b: e.reciprocal(rec[:, :], den[:, :]), A("vector", "den", t))
            add("vector", f + 10, ("norm", t), lambda e, b: e.scalar_tensor_tensor(
                out=onrm[:, :].rearrange("p (h d) -> p h d", d=HD), in0=osb[:, :, 0:HD], scalar=1.0 / ASCALE,
                in1=bcast(rec[:, :], 2, HD), op0=ALU.mult, op1=ALU.mult),
                A("vector", "rec", t), prev_t("tensor", "o_T"))
            add("tensor", f + 11, ("o_T", t), lambda e, b: [e.transpose(
                R3[:, k * P:(k + 1) * P], onrm[:, k * P:(k + 1) * P], ident[:, :]) for k in range(KD)][-1],
                A("vector", "norm", t), A("vector", "st1", t), S("gpsimd", "id"))
            oT = R3[:, 0:D].rearrange("p (k n) -> p k n", k=KD)
            add("scalar", f + 11, ("o_hi", t), lambda e, b, tok=tok, oT=oT: e.activation(xo[0][:, :, tok], oT, ACT.Copy),
                A("tensor", "o_T", t))
            add("vector", f + 11, ("o_lo", t), lambda e, b, tok=tok, oT=oT: e.tensor_tensor(
                xo[1][:, :, tok], oT, xo[0][:, :, tok].bitcast(F32), ALU.subtract), A("scalar", "o_hi", t))

        z = 2 + 8 * (NT - 1) + 12

        def proj(e, b):
            for m_ in range(KD):
                n = 0
                for k in range(KD):
                    for wi, xi in ((0, 0), (1, 0), (0, 1)):
                        mm = e.matmul(BK[m_][:, :], wout_p[wi][:, k, m_ * P:(m_ + 1) * P], xo[xi][:, k, :],
                                      start=(n == 0), stop=(n == 3 * KD - 1))
                        n += 1
            return mm
        add("tensor", z, ("proj",), proj, A("scalar", "o_hi", NT - 1), A("vector", "o_lo", NT - 1),
            S("vector", "wout_lo"))
        for k in range(KD):
            add("vector", z, ("x1", k), lambda e, b, k=k: e.tensor_tensor(x1[:, k, :], BK[k][:, :], xraw[:, k, :], ALU.add),
                A("tensor", "proj"), Mb("scalar", "x2_hi", k), Mb("vector", "x2_lo", k))
        add("sync", z, None, lambda e, b: e.dma_start(x1_scr.rearrange("(k p) n -> p k n", p=P), x1[:, :, :])
            .then_inc(dsem["x1_out"], 16), A("vector", "x1", KD - 1), dma("x1_in", 1, 1, 1))
        add("tensor", z + 1, ("mean2",), lambda e, b: [e.matmul(
            R2[:, :], mean_w[:, :], x1[:, k, :], start=(k == 0), stop=(k == KD - 1)) for k in range(KD)][-1],
            A("vector", "x1", 0), A("vector", "x1", 1))
        for k in range(KD):
            add("vector", z + 2, ("xc", k), lambda e, b, k=k: e.tensor_tensor(
                x1[:, k, :], x1[:, k, :], R2[:, :], ALU.subtract), A("tensor", "mean2"), dma("x1_out", 1, 1))
            add("scalar", z + 2, ("sq", k), lambda e, b, k=k: e.activation(sq[:, :], x1[:, k, :], ACT.Square),
                A("vector", "xc", k), A("tensor", "var2", k - 1) if k else Ab("tensor", "v2T"))
            add("tensor", z + 3, ("var2", k), lambda e, b, k=k: e.matmul(
                R3[:, :], mean_w[:, :], sq[:, :], start=(k == 0), stop=(k == KD - 1)),
                A("scalar", "sq", k), A("vector", "x1", 1))
        add("scalar", z + 4, ("v2r",), lambda e, b: e.activation(sq[:, :], R3[:, :], ACT.Copy),
            A("tensor", "var2", 1))
        add("tensor", z + 4, ("v2T",), lambda e, b: [e.transpose(
            R2[:, t * P:(t + 1) * P], sq[:, t * P:(t + 1) * P], ident[:, :]) for t in range(NT)][-1],
            A("scalar", "v2r"), A("vector", "xc", KD - 1))
        add("vector", z + 4, ("v2n",), lambda e, b: e.tensor_scalar(v2n[:, :], R2[:, 0::P], EPS, None, ALU.add),
            A("tensor", "v2T"))
        add("gpsimd", z + 4, ("r2n",), lambda e, b: e.tensor_tensor(r2n[:, :], v2n[:, :], mhalf[:, :], ALU.pow),
            A("vector", "v2n"))
        add("tensor", z + 5, ("rstd2",), lambda e, b: [e.transpose(
            R3[:, t * P:(t + 1) * P], r2n[:, t:t + 1].broadcast_to([P, P]), ident[:, :]) for t in range(NT)][-1],
            A("gpsimd", "r2n"))
        for k in range(KD):
            add("vector", z + 5, ("ln2", k), lambda e, b, k=k: e.tensor_tensor(
                x1[:, k, :], x1[:, k, :], R3[:, :], ALU.mult), A("tensor", "rstd2"))

        add("tensor", z + 5, ("logit",), lambda e, b: [e.matmul(
            R2[0:E, :], wr_sb[:, k, :], x1[:, k, :], start=(k == 0), stop=(k == KD - 1)) for k in range(KD)][-1],
            A("vector", "ln2", 0), A("vector", "ln2", 1), ("once", "c_wr", 1, 0))
        add("scalar", z + 6, ("lgT",), lambda e, b: e.activation(rt[0:E, :], R2[0:E, :], ACT.Copy),
            A("tensor", "logit"), dma("w_out", 1, 1, 1), S("vector", "z_rt"))
        add("tensor", z + 6, ("lg",), lambda e, b: [e.transpose(
            R3[:, t * P:(t + 1) * P], rt[:, t * P:(t + 1) * P], ident[:, :]) for t in range(NT)][-1],
            A("scalar", "lgT"), A("vector", "ln2", 1))
        r_ = {n: v[:, :, :] for n, v in R.items()}
        q_ = {n: v[:, :] for n, v in R1.items()}
        lg = R3[:, :].rearrange("p (t n) -> p t n", n=P)[:, :, 0:E]
        io = bcast(iota[:, :], 1, NT)
        steps = [
            ("vector", "z", lambda e: e.tensor_scalar(r_["z"], lg, rtemp[:, 0:1], None, ALU.mult)),
            ("scalar", "th", lambda e: e.activation(r_["th"], r_["z"], ACT.Tanh, scale=0.5)),
            ("vector", "inh", lambda e: e.tensor_scalar(r_["inh"], r_["th"], 0.5, 0.5, ALU.mult, ALU.add)),
            ("vector", "zone", lambda e: e.tensor_scalar(r_["zone"], r_["inh"], G_LOWER, None, ALU.is_ge)),
            ("vector", "zone2", lambda e: e.scalar_tensor_tensor(
                out=r_["zone2"], in0=r_["inh"], scalar=G_UPPER, in1=r_["zone"], op0=ALU.is_le, op1=ALU.mult)),
            ("vector", "nd0", lambda e: e.tensor_scalar(r_["nd"], r_["inh"], G_CENTER, None, ALU.subtract)),
            ("vector", "dist", lambda e: e.scalar_tensor_tensor(
                out=r_["dist"], in0=r_["nd"], scalar=-1.0, in1=r_["nd"], op0=ALU.mult, op1=ALU.max)),
            ("scalar", "e1", lambda e: e.activation(r_["e1"], r_["dist"], ACT.Exp, scale=-1.0 / 0.1)),
            ("scalar", "fb", lambda e: e.activation(r_["fb"], r_["dist"], ACT.Exp, scale=-1.0 / 0.3)),
            ("vector", "w0", lambda e: e.tensor_tensor(r_["w0"], r_["e1"], r_["zone2"], ALU.mult)),
            ("vector", "ws", lambda e: e.tensor_reduce(q_["ws"], r_["w0"], AX.X, ALU.add)),
            ("vector", "no", lambda e: e.tensor_scalar(q_["no"], q_["ws"], 1e-8, None, ALU.is_lt)),
            ("vector", "yes", lambda e: e.tensor_scalar(q_["yes"], q_["ws"], 1e-8, None, ALU.is_ge)),
            ("vector", "m", lambda e: e.tensor_reduce(q_["m"], r_["dist"], AX.X, ALU.min)),
            ("vector", "eq", lambda e: e.tensor_tensor(r_["eq"], r_["dist"], bcast(q_["m"], 2, E), ALU.not_equal)),
            ("vector", "c", lambda e: e.scalar_tensor_tensor(
                out=r_["c"], in0=r_["eq"], scalar=99.0, in1=io, op0=ALU.mult, op1=ALU.add)),
            ("vector", "ix", lambda e: e.tensor_reduce(q_["ix"], r_["c"], AX.X, ALU.min)),
            ("vector", "s1", lambda e: e.tensor_tensor(r_["s1"], io, bcast(q_["ix"], 2, E), ALU.is_equal)),
            ("vector", "nd", lambda e: e.scalar_tensor_tensor(
                out=r_["nd"], in0=r_["s1"], scalar=9.0, in1=r_["dist"], op0=ALU.mult, op1=ALU.add)),
            ("vector", "m2", lambda e: e.tensor_reduce(q_["m2"], r_["nd"], AX.X, ALU.min)),
            ("vector", "eq2", lambda e: e.tensor_tensor(r_["eq"], r_["nd"], bcast(q_["m2"], 2, E), ALU.not_equal)),
            ("vector", "c2", lambda e: e.scalar_tensor_tensor(
                out=r_["c"], in0=r_["eq"], scalar=99.0, in1=io, op0=ALU.mult, op1=ALU.add)),
            ("vector", "ix2", lambda e: e.tensor_reduce(q_["ix2"], r_["c"], AX.X, ALU.min)),
            ("vector", "s2", lambda e: e.tensor_tensor(r_["s2"], io, bcast(q_["ix2"], 2, E), ALU.is_equal)),
            ("vector", "s12", lambda e: e.tensor_tensor(r_["s1"], r_["s1"], r_["s2"], ALU.add)),
            ("vector", "fw", lambda e: e.tensor_tensor(r_["fw"], r_["fb"], r_["s1"], ALU.mult)),
            ("vector", "fs", lambda e: e.tensor_reduce(q_["fs"], r_["fw"], AX.X, ALU.add)),
            ("vector", "fs1", lambda e: e.tensor_scalar(q_["fs"], q_["fs"], 1e-8, None, ALU.max)),
            ("vector", "fs2", lambda e: e.reciprocal(q_["fs"], q_["fs"])),
            ("vector", "fw1", lambda e: e.tensor_tensor(r_["fw"], r_["fw"], bcast(q_["fs"], 2, E), ALU.mult)),
            ("vector", "fw2", lambda e: e.tensor_tensor(r_["fw"], r_["fw"], bcast(q_["no"], 2, E), ALU.mult)),
            ("vector", "w1", lambda e: e.tensor_tensor(r_["w0"], r_["w0"], bcast(q_["yes"], 2, E), ALU.mult)),
            ("vector", "w", lambda e: e.tensor_tensor(r_["w"], r_["w0"], r_["fw"], ALU.add)),
            ("vector", "w2", lambda e: e.tensor_reduce(q_["w2"], r_["w"], AX.X, ALU.add)),
            ("vector", "w3", lambda e: e.tensor_scalar(q_["w2"], q_["w2"], 1e-8, 2.0, ALU.max, ALU.mult)),
            ("vector", "w4", lambda e: e.reciprocal(q_["w2"], q_["w2"])),
            ("vector", "wo", lambda e: e.tensor_tensor(r_["wo"], r_["w"], bcast(q_["w2"], 2, E), ALU.mult)),
        ]
        last = A("tensor", "lg")
        for n, (eng, name, fn) in enumerate(steps):
            waits = [last, S("vector", "rtemp"), Ab("tensor", "w_T")] if n == 0 else [last]
            if name == "w0":
                waits.append(A("scalar", "e1"))
            add(eng, z + 6.1 + n * 0.04, (name,), lambda e, b, fn=fn: fn(e), *waits)
            last = A(eng, name)
        add("tensor", z + 8, ("w_T",), lambda e, b: [e.transpose(
            R2[0:E, t * P:(t + 1) * P], R["wo"][:, t, :], ident[:, :]) for t in range(NT)][-1],
            A("vector", "wo"), A("scalar", "lgT"))
        add("scalar", z + 8, ("wt",), lambda e, b: e.activation(rt[0:E, :], R2[0:E, :], ACT.Copy), A("tensor", "w_T"))
        add("sync", z + 8, None, lambda e, b: e.dma_start(w_scr, rt[0:E, :]).then_inc(dsem["w_out"], 16),
            A("scalar", "wt"), *[dma(f"wb{i}", len(range(i, E, NWB)), len(range(i, E, NWB)), 1) for i in range(NWB)])

        add = moe.add
        for k in range(KD):
            add("scalar", -1, ("x2_hi", k), lambda e, b, k=k: e.activation(x2[0][:, k, :], x1[:, k, :], ACT.Copy),
                A("vector", "ln2", k), Mb("tensor", "up", UNITS - 1))
            add("vector", -1, ("x2_lo", k), lambda e, b, k=k: e.tensor_tensor(
                x2[1][:, k, :], x1[:, k, :], x2[0][:, k, :].bitcast(F32), ALU.subtract), M("scalar", "x2_hi", k))
        add("sync", 1, None, lambda e, b: e.dma_start(x1r[:, :, :], x1_scr.rearrange("(k p) n -> p k n", p=P))
            .then_inc(dsem["x1_in"], 16), dma("x1_out", 1, 1), dma("y_out", 1, 1, 1), S("vector", "wout_lo"))
        for e_ in range(E):
            s, n = e_ % NWB, e_ // NWB + 1
            cnt = len(range(s, E, NWB))
            if e_ < NWB:
                last_use = max(x_ for x_ in range(E) if x_ % NWB == s)
                free = [Mb("vector", "gw", 2 * last_use + 1)] + last_slabs
            else:
                free = [M("vector", "gw", 2 * (e_ - NWB) + 1)]
            add("sync", 0 if e_ < NWB else 6 * (e_ - NWB) + 7, None, lambda e, b, e_=e_, s=s: e.dma_start(
                wb[:, s, :], w_scr[e_:e_ + 1, :].broadcast_to([P, B])).then_inc(dsem[f"wb{s}"], 16),
                dma("w_out", 1, 1), *free)

        def three(e, out, w, wsel, xs, xsel, start, stop):
            todo = [(wi, xi, k) for wi, xi in ((0, 0), (1, 0), (0, 1)) for k in range(len(wsel))]
            for n, (wi, xi, k) in enumerate(todo):
                m = e.matmul(out, wsel[k](w[wi]), xsel[k](xs[xi]), start=start and n == 0,
                             stop=stop and n == len(todo) - 1, skip_group_check=not (start and stop))
            return m

        for u in range(UNITS):
            e_, m_ = u // KI, u % KI
            c = slice(m_ * P, (m_ + 1) * P)
            hs = u % 2
            prv = (lambda eng, ev, d=1: M(eng, ev, u - d) if u >= d else Mb(eng, ev, UNITS + u - d))
            wsel = [lambda w, k=k, e_=e_, c=c: w[:, e_, k, c] for k in range(KD)]
            xsel = [lambda x_, k=k: x_[:, k, :] for k in range(KD)]
            add("tensor", 3 * u, ("gate", u), lambda e, b, wsel=wsel, xsel=xsel: three(
                e, G[:, :], wg_p, wsel, x2, xsel, True, True),
                prv("vector", "g"), M("scalar", "x2_hi", KD - 1), M("vector", "x2_lo", KD - 1), *last_slabs)
            add("tensor", 3 * u + 1, ("up", u), lambda e, b, wsel=wsel, xsel=xsel: three(
                e, U[:, :], wu_p, wsel, x2, xsel, True, True), prv("vector", "h"))
            add("scalar", 3 * u + .5, ("tanh", u), lambda e, b, hs=hs: e.activation(hb[:, hs, :], G[:, :], ACT.Tanh, scale=0.5),
                M("tensor", "gate", u), prv("gpsimd", "h_lo", 2), prv("scalar", "h_hi", 2))
            add("vector", 3 * u + .5, ("g", u), lambda e, b, hs=hs: e.scalar_tensor_tensor(
                out=hb[:, hs, :], in0=hb[:, hs, :], scalar=1.0, in1=G[:, :], op0=ALU.add, op1=ALU.mult),
                M("scalar", "tanh", u))
            add("vector", 3 * u + 1, ("gw", u), lambda e, b, hs=hs, e_=e_: e.tensor_tensor(
                hb[:, hs, :], hb[:, hs, :], wb[:, e_ % NWB, :], ALU.mult),
                M("vector", "g", u), dma(f"wb{e_ % NWB}", len(range(e_ % NWB, E, NWB)), e_ // NWB + 1))
            add("vector", 3 * u + 1.5, ("h", u), lambda e, b, hs=hs: e.tensor_tensor(
                hb[:, hs, :], hb[:, hs, :], U[:, :], ALU.mult), M("vector", "gw", u), M("tensor", "up", u))
            add("scalar", 3 * u + 2, ("h_hi", u), lambda e, b, hs=hs: e.activation(h_p[0][:, hs, :], hb[:, hs, :], ACT.Copy),
                M("vector", "h", u), prv("tensor", "down", 2))
            add("gpsimd", 3 * u + 2, ("h_lo", u), lambda e, b, hs=hs: e.tensor_tensor(
                h_p[1][:, hs, :], hb[:, hs, :], h_p[0][:, hs, :].bitcast(F32), ALU.subtract),
                M("scalar", "h_hi", u), prv("tensor", "down", 2))

            def down(e, b, u=u, e_=e_, m_=m_, hs=hs):
                for wi, hi in ((0, 0), (1, 0), (0, 1)):
                    for d in range(KD):
                        mm = e.matmul(Y[d][:, :], wd_p[wi][:, e_, m_, d * P:(d + 1) * P], h_p[hi][:, hs, :],
                                      start=(u == 0 and (wi, hi) == (0, 0)),
                                      stop=(u == UNITS - 1 and hi == 1), skip_group_check=True)
                return mm
            waits = [M("scalar", "h_hi", u), M("gpsimd", "h_lo", u)]
            if u == 0:
                waits += [Mb("vector", "y", k) for k in range(KD)]
            add("tensor", 3 * (u + 1) + 2, ("down", u), down, *waits)
        for k in range(KD):
            add("vector", SLOTS + 3, ("y", k), lambda e, b, k=k: e.tensor_tensor(
                x1r[:, k, :], Y[k][:, :], x1r[:, k, :], ALU.add), M("tensor", "down", UNITS - 1), dma("x1_in", 1, 1))
        add("sync", SLOTS + 3, None, lambda e, b: e.dma_start(
            outT[:, bass.ds(b, B)].rearrange("(k p) n -> p k n", p=P), x1r[:, :, :]).then_inc(dsem["y_out"], 16),
            M("vector", "y", KD - 1))

        for part in parts.values():
            part.close()

        def emit(engine, eng, which, blocks):
            merged = [(slot, n, name, event, fn, waits) for n, name in enumerate(which)
                      for slot, event, fn, waits in parts[name].ops[engine]]
            merged.sort(key=lambda x_: x_[0])
            seen = {}
            rows = {n: b * B if isinstance(b, int) else eng.snap(b * B) for n, b in blocks.items()} \
                if engine == "sync" else {}
            for _, _, name, event, fn, waits in merged:
                b = blocks[name]
                arg = rows[name] if engine == "sync" else b
                todo = []
                for kind, producer, w_event, back in waits:
                    if kind == "once":
                        sm, per, rel = dsem[producer], 0, 16 * w_event
                    elif kind == "dma":
                        (n, k) = w_event
                        sm, per, rel = dsem[producer], 16 * n, 16 * (k + ((producer == "y_out") - back) * n)
                    else:
                        n = parts[kind].count[producer] if kind != "setup" else 0
                        sm, per = sems[kind, producer], n
                        rel = parts[kind].number[producer, w_event] + ((kind == "moe") - back) * n
                    value = b * per + rel
                    if isinstance(value, int):
                        if value <= 0:
                            continue
                        key, known = sm.name, value
                    else:
                        key, known = (sm.name, name, per == 0), rel
                    if seen.get(key, 0) < known or key not in seen:
                        seen[key] = known
                        todo.append((sm, value))
                for n, (sm, value) in enumerate(todo):
                    eng.wait_ge(sm, value)
                    if engine == "sync" and not isinstance(b, int) and (n + 1 < len(todo)):
                        eng.sem_inc(carrier, 1)
                ins = fn(eng, arg)
                if event is not None and engine != "sync":
                    ins.then_inc(sems[name, engine], 1)

        def program(engine):
            def run(eng):
                if engine != "sync":
                    eng.sem_inc(sems["moe", engine], moe.count[engine])
                else:
                    eng.sem_inc(dsem["y_out"], 16)
                emit(engine, eng, ("setup", "att"), {"setup": 0, "att": 0})
                with eng.Fori(1, NB) as i:
                    emit(engine, eng, ("att", "moe"), {"att": i, "moe": i - 1})
                emit(engine, eng, ("moe",), {"moe": NB - 1})
                if engine == "sync":
                    for n in ("x1_out", "w_out", "y_out"):
                        eng.wait_ge(dsem[n], 16 * (NB + (n == "y_out")))
            return run

        block = ctx.enter_context(nc.Block())
        block.tensor(program("tensor"))
        block.scalar(program("scalar"))
        block.vector(program("vector"))
        block.gpsimd(program("gpsimd"))
        block.sync(program("sync"))


def kernel(**inputs):
    import concourse.bacc as bacc
    from concourse.bass_utils import run_bass_kernel_spmd

    x = np.asarray(inputs["L0_attn_x"])
    inv_freq = (np.float32(1.0) / np.power(np.float32(10000.0), np.arange(HALF, dtype=np.float32) / np.float32(HALF)))
    ang = (np.arange(N, dtype=np.float32)[:, None] * inv_freq.astype(np.float32)[None, :]).astype(np.float64)
    cos, sin = (f(ang).astype(np.float32) * np.float32(SCALE) for f in (np.cos, np.sin))
    arrays = {
        "x": np.ascontiguousarray(x[0]),
        "xT": np.ascontiguousarray(x[0].T),
        "w_qkv": np.ascontiguousarray(inputs["L0_attn_w_qkv"]),
        "w_out": np.ascontiguousarray(inputs["L0_attn_w_out"]),
        "Wg": np.ascontiguousarray(inputs["L0_ffn_Wg"]),
        "Wu": np.ascontiguousarray(inputs["L0_ffn_Wu"]),
        "Wd": np.ascontiguousarray(inputs["L0_ffn_Wd"]),
        "Wr": np.ascontiguousarray(inputs["L0_ffn_Wr"]),
        "temperature": np.ascontiguousarray(inputs["L0_ffn_temperature"]),
        "tab": np.concatenate([cos, -sin, sin], axis=1),
    }
    nc = bacc.Bacc("TRN2", target_bir_lowering=False, num_devices=1)
    args = [nc.dram_tensor(n, list(a.shape), F32, kind="ExternalInput").ap() for n, a in arrays.items()]
    args.append(nc.dram_tensor("outT", [D, N], F32, kind="ExternalOutput").ap())
    args.append(nc.dram_tensor("w_scr", [E, B], F32, kind="Internal").ap())
    args.append(nc.dram_tensor("x1_scr", [D, B], F32, kind="Internal").ap())
    build(nc, *args)
    r = run_bass_kernel_spmd(nc, [arrays], core_ids=[0])
    return np.ascontiguousarray(r.results[0]["outT"].T)[None]
```

```python
from contextlib import ExitStack

import numpy as np

import concourse.bass as bass
from concourse import mybir

F32 = mybir.dt.float32
F32R = mybir.dt.float32r
F16 = mybir.dt.float16
BF16 = mybir.dt.bfloat16
ALU = mybir.AluOpType
ACT = mybir.ActivationFunctionType
AX = mybir.AxisListType

P = 128
N, D = 4096, 256
B = 512
NB = N // B
NT = B // P
KD = D // P
H, HD = 16, 16
HALF = HD // 2
NP = H // 2
E, I = 8, 256
KI = I // P
UNITS = E * KI
W1 = HD + 1
WV = 3 * W1
SCALE = float(HD ** -0.25)
EPS = 1e-5
ASCALE = 1.0 / 16.0
G_CENTER = 1.0 / float(np.e)
G_LOWER = 0.5 - float(np.log(4.0 / 3.0))
G_UPPER = 0.5
SLOTS = 3 * UNITS
TILE = (4, 13, 22, 31)
Z0 = 49.5
M0 = 66
NWB = 3
PLACE = {
    "setup": {
        "load_w_qkv": 0, "load_w_out": 0, "load_Wr": 0, "load_temperature": 0, "ones": 0, "mhalf": 0,
        "rtemp": 0, "rtemp2": 0, "id0": 0, "mask0": 0, "id": 0, "mask": 0, "iota_i": 0, "iota": 0, "id16": 0,
        "z_qbd": 0, "z_vx": 0, "one_vx": 0, "z_sx": 0, "z_ss": 0, "colmean": 0, "wc": 1, "wqkv_hi": 2.5,
        "wqkv_lo": 3, "wout_hi": 1, "wout_lo": 7.25, "load_slab": 14, "slab_hi": 10.25, "slab_lo": 11.75,
    },
    "att": {
        "load_x": 2.75, "load_tab": 9.5, "x_hi": 2.25, "x_lo": 2.5, "load_xnat": -4, "bn": -4, "mv": -2,
        "ve": -0.25, "rstd1": 0.25, "qkv": 0, "qk": 2.5, "v": 2.5, "cos": 1.5, "sin1": 2.75, "sin2": 3,
        "rope": 3.25, "exp": 4.75, "relu": 4.75, "phi": 5.25, "q_hi": 5.5, "k_hi": 6, "q_lo": 6.25,
        "k_lo": 6.25, "v1": 5.25, "vr": 5, "v2": 6, "v3": 6.25, "k_T": 8.5, "q_T": 7.5, "kT": 8, "qT0": 8.5,
        "qT1": 7.75, "qk0": 8.75, "qk1": 9, "qk2": 9.25, "qk3": 11, "mask0": 9.5, "mask1": 9.75, "mask2": 10.5,
        "mask3": 11.5, "a_hi0": 10.5, "a_hi1": 10.5, "a_hi2": 11.75, "a_hi3": 12.25, "a_lo0": 11.75,
        "a_lo1": 11.75, "a_lo2": 12.25, "a_lo3": 12.5, "av0": 12, "av1": 14.25, "o0": 12.5, "o1": 14,
        "state": 14.5, "st0_0": 15.5, "st0_1": 15.25, "st1_0": 14.5, "st1_1": 14.5, "ss": 16, "s1": 18,
        "sr": 18.25, "s2": 20.5, "s3": 21, "den": 14.1, "rec": 14.35, "norm": 14.6, "o_T": 16, "o_hi": 15.5,
        "o_lo": 15.75, "proj": -1.25, "x1": -1.75, "store_x1": 5, "mean2": 2, "xc": 2.5, "sq": 3.5,
        "var2": 3.75, "logit": 4.5, "v2n": 5.5, "r2n": 6.5, "rstd2": 7.25, "ln2": 8.5, "router": 9, "w_T": 16,
        "wt": 16, "store_w": 16, "x2_hi": -1.1, "x2_lo": -1.1,
    },
    "moe": {
        "load_x1": 13.5, "load_w": 1, "gate": 0.25, "up": 0.5, "tanh": 0.75, "g": 1.25, "h": 1.75, "gw": 2.25,
        "h_hi": 4.5, "h_lo": 5.5, "down": 8.25, "y": 6, "store_y": 9,
    },
}


class Part:

    def __init__(self, name):
        self.name = name
        self.ops = {e: [] for e in ENGINES}
        self.number = {}
        self.count = {}

    def add(self, engine, slot, event, fn, *waits):
        slot += PLACE[self.name][event if isinstance(event, str) else event[0]]
        late = int(slot // SLOTS) if self.name != "setup" else 0
        self.ops[engine].append((slot, late, event, fn, waits))

    def close(self):
        for engine, ops in self.ops.items():
            ops.sort(key=lambda op: op[0])
            for _, late, event, _, _ in ops:
                if isinstance(event, tuple):
                    n = self.count.get((late, engine), 0) + 1
                    self.count[late, engine] = n
                    self.number[engine, event] = late, n


ENGINES = ("tensor", "scalar", "vector", "gpsimd", "sync")


def bcast(ap, axis, n):
    ap = ap.unsqueeze(axis)
    shape = list(ap.shape)
    shape[axis] = n
    return ap.broadcast_to(shape)


def build(nc, x, xT, w_qkv, w_out, Wg, Wu, Wd, Wr, temperature, tab, outT, w_scr, x1_scr):
    ctx = ExitStack()

    def sb(name, shape, dt=F32):
        return ctx.enter_context(nc.sbuf_tensor(name, shape, dt))

    def sem(name):
        return ctx.enter_context(nc.semaphore(name))

    with ctx:
        ident = sb("ident", [P, P])
        ident16 = sb("ident16", [P, P], F16)
        cmask = sb("cmask", [P, P])
        mean_w = sb("mean_w", [P, P])
        iota = sb("iota", [P, E])
        iota_i = sb("iota_i", [P, E], mybir.dt.int32)
        temp = sb("temp", [P, 1])
        rtemp = sb("rtemp", [P, 1])
        mhalf = sb("mhalf", [P, NT])
        wqkv_p = [sb(f"wqkv_{s}", [P, KD, 3 * D], F32R) for s in ("hi", "lo")]
        wout_p = [sb(f"wout_{s}", [P, KD, D], F32R) for s in ("hi", "lo")]
        wg_p = [sb(f"wg_{s}", [P, E, KD, I], F32R) for s in ("hi", "lo")]
        wu_p = [sb(f"wu_{s}", [P, E, KD, I], F32R) for s in ("hi", "lo")]
        wd_p = [sb(f"wd_{s}", [P, E, KI, D], F32R) for s in ("hi", "lo")]
        wr_sb = sb("wr_sb", [P, KD, E])
        xraw = sb("xraw", [P, KD, B])
        xnat = sb("xnat", [P, 2, D])
        tabs = sb("tabs", [P, NT, 3 * HALF])
        xo = [sb(f"xo_{s}", [P, KD, B], F32R) for s in ("hi", "lo")]
        bst = sb("bst", [P, 6])
        idle = sb("idle", [P, 1])
        ve = sb("ve", [P, NT])
        v2n = sb("v2n", [P, NT])
        r2n = sb("r2n", [P, NT])
        mv = sb("mv", [P, NT, 2])
        rstd1 = sb("rstd1", [P, NT])
        qk = sb("qk", [P, 2 * D])
        rop = sb("rop", [P, 2 * D])
        rop2 = sb("rop2", [P, 2 * D])
        ex = sb("ex", [P, 2 * D])
        vs = sb("vs", [P, D])
        stack = sb("stack", [P, 2 * H, 4, HD], F16)
        kT = sb("kT", [P, NP, P], F16)
        qbd = sb("qbd", [P, NP, 2, P], F16)
        vx = sb("vx", [P, H, 3, W1], BF16)
        am = sb("am", [P, 2, 4 * P])
        a_p = [sb(f"a_{s}", [P, H, P], F16) for s in ("hi", "lo")]
        osb = sb("osb", [P, H, W1])
        den = sb("den", [P, H])
        rec = sb("rec", [P, H])
        onrm = sb("onrm", [P, D])
        st_d = sb("st_d", [P, NP, W1])
        st_s = sb("st_s", [P, NP, W1])
        st_r = sb("st_r", [P, NP, W1])
        st_x = sb("st_x", [P, NP, 3, W1], BF16)
        x1 = sb("x1", [P, KD, B])
        sq = sb("sq", [P, B])
        rt = sb("rt", [E, B])
        R = {n: sb(f"r_{n}", [P, NT, E]) for n in
             ("z", "th", "inh", "zone", "zone2", "dist", "e1", "fb", "w0", "eq", "c", "s1", "nd", "s2", "fw", "w", "wo")}
        R1 = {n: sb(f"q_{n}", [P, NT]) for n in ("ws", "no", "yes", "m", "ix", "m2", "ix2", "fs", "w2")}
        x2 = [sb(f"x2_{s}", [P, KD, B], F32R) for s in ("hi", "lo")]
        x1r = sb("x1r", [P, KD, B])
        wb = sb("wb", [P, NWB, B])
        hb = sb("hb", [P, 2, B])
        h_p = [sb(f"h_{s}", [P, 2, B], F32R) for s in ("hi", "lo")]
        G, U, Y0, Y1, R0, R1b, R2, R3 = (
            ctx.enter_context(nc.psum_tensor(n, [P, 512], F32))
            for n in ("gate", "up", "y0", "y1", "front0", "front1", "back0", "back1"))
        Y, FR, BK = [Y0, Y1], [R0, R1b], [R2, R3]

        dma_names = ("c_temp", "c_wr", "c_wqkv", "c_wout", "x_raw", "x_nat0", "x_nat1", "tab", "x1_out", "w_out",
                     "x1_in", "y_out") + tuple(f"wb{i}" for i in range(NWB)) + tuple(f"slab{i}" for i in range(NWB))
        carrier = sem("carrier")
        dsem = {n: sem(f"dma_{n}") for n in dma_names}

        setup, att, moe = (Part(n) for n in ("setup", "att", "moe"))
        parts = {"setup": setup, "att": att, "moe": moe}

        def at(part, engine, *event):
            return (part, engine, event, 0)

        def before(part, engine, *event):
            return (part, engine, event, 1)

        def dma(name, per_block, k, back=0):
            return ("dma", name, (per_block, k), back)

        def S(engine, *event):
            return at("setup", engine, *event)

        add = setup.add
        wq_raw = wb[:, :, :].rearrange("p a b -> p (a b)").rearrange("p (k n) -> p k n", k=KD)
        wo_raw = x1r[:, 0, :].rearrange("p (k n) -> p k n", k=KD)
        add("sync", 0, "load_w_qkv", lambda e, b: e.dma_start(wq_raw, w_qkv.rearrange("(k p) n -> p k n", p=P))
            .then_inc(dsem["c_wqkv"], 16))
        add("sync", 0, "load_w_out", lambda e, b: e.dma_start(wo_raw, w_out.rearrange("(k p) n -> p k n", p=P))
            .then_inc(dsem["c_wout"], 16))
        add("sync", 0, "load_Wr", lambda e, b: e.dma_start(wr_sb[:, :, :], Wr.rearrange("(k p) n -> p k n", p=P))
            .then_inc(dsem["c_wr"], 16))
        add("sync", 0, "load_temperature", lambda e, b: e.dma_start(temp[:, :], temperature.rearrange("(a n) -> a n", a=1)
                                                      .broadcast_to([P, 1])).then_inc(dsem["c_temp"], 16))
        add("vector", 0, ("ones",), lambda e, b: e.memset(mean_w[:, :], 1.0 / D))
        add("vector", 0, ("mhalf",), lambda e, b: e.memset(mhalf[:, :], -0.5))
        add("vector", 0, ("rtemp",), lambda e, b: e.reciprocal(rtemp[:, :], temp[:, :]), ("once", "c_temp", 1, 0))
        add("vector", 0, ("rtemp2",), lambda e, b: e.tensor_scalar(rtemp[:, :], rtemp[:, :], 0.5, None, ALU.mult),
            S("vector", "rtemp"))
        add("gpsimd", 0, ("id0",), lambda e, b: e.memset(ident[:, :], 0.0))
        add("gpsimd", 0, ("mask0",), lambda e, b: e.memset(cmask[:, :], ASCALE))
        add("gpsimd", 0, ("id",), lambda e, b: e.affine_select(
            out=ident[:, :], in_=ident[:, :], compare_op=ALU.not_equal, fill=1.0, base=0,
            pattern=[[-1, P]], channel_multiplier=1), S("gpsimd", "id0"))
        add("gpsimd", 0, ("mask",), lambda e, b: e.affine_select(
            out=cmask[:, :], in_=cmask[:, :], compare_op=ALU.is_ge, fill=0.0, base=0,
            pattern=[[1, P]], channel_multiplier=-1), S("gpsimd", "mask0"))
        add("gpsimd", 0, ("iota_i",), lambda e, b: e.iota(iota_i[:, :], pattern=[[1, E]], base=0, channel_multiplier=0))
        add("vector", 0, ("iota",), lambda e, b: e.tensor_copy(iota[:, :], iota_i[:, :]), S("gpsimd", "iota_i"))
        add("vector", 0, ("id16",), lambda e, b: e.tensor_copy(ident16[:, :], ident[:, :]), S("gpsimd", "id"))
        add("vector", 0, ("z_qbd",), lambda e, b: e.memset(qbd[:, :, :, :].rearrange("p a b c -> p (a b c)"), 0.0))
        add("vector", 0, ("z_vx",), lambda e, b: e.memset(vx[:, :, :, :].rearrange("p a b c -> p (a b c)"), 0.0))
        add("vector", 0, ("one_vx",), lambda e, b: e.memset(vx[:, :, 0, HD], 1.0), S("vector", "z_vx"))
        add("vector", 0, ("z_sx",), lambda e, b: e.memset(st_x[:, :, :, :].rearrange("p a b c -> p (a b c)"), 0.0))
        add("vector", 0, ("z_ss",), lambda e, b: e.memset(st_s[:, :, :].rearrange("p a b -> p (a b)"), 0.0))

        def col_means(e, b):
            for k in range(KD):
                e.matmul(R0[:, :], mean_w[:, :], wq_raw[:, k, 0:2 * D], start=(k == 0), stop=(k == KD - 1))
            for k in range(KD):
                m = e.matmul(R1b[:, 0:D], mean_w[:, :], wq_raw[:, k, 2 * D:], start=(k == 0), stop=(k == KD - 1))
            return m
        add("tensor", 0, ("colmean",), col_means, S("vector", "ones"), ("once", "c_wqkv", 1, 0))
        for k in range(KD):
            add("vector", 0, ("wc", k, 0), lambda e, b, k=k: e.tensor_tensor(
                wq_raw[:, k, 0:2 * D], wq_raw[:, k, 0:2 * D], R0[:, :], ALU.subtract), S("tensor", "colmean"))
            add("vector", 0, ("wc", k, 1), lambda e, b, k=k: e.tensor_tensor(
                wq_raw[:, k, 2 * D:], wq_raw[:, k, 2 * D:], R1b[:, 0:D], ALU.subtract), S("tensor", "colmean"))
            add("scalar", 0, ("wqkv_hi", k), lambda e, b, k=k: e.activation(
                wqkv_p[0][:, k, :], wq_raw[:, k, :], ACT.Copy), S("vector", "wc", k, 0), S("vector", "wc", k, 1))
            add("vector", 0, ("wqkv_lo", k), lambda e, b, k=k: e.tensor_tensor(
                wqkv_p[1][:, k, :], wq_raw[:, k, :], wqkv_p[0][:, k, :].bitcast(F32), ALU.subtract),
                S("scalar", "wqkv_hi", k))
        add("scalar", 0, ("wout_hi",), lambda e, b: e.activation(wout_p[0][:, :, :], wo_raw, ACT.Copy),
            ("once", "c_wout", 1, 0))
        add("vector", 0, ("wout_lo",), lambda e, b: e.tensor_tensor(
            wout_p[1][:, :, :], wo_raw, wout_p[0][:, :, :].bitcast(F32), ALU.subtract), S("scalar", "wout_hi"))

        slabs = [(src, dst, ex_) for ex_ in range(E) for src, dst in ((Wg, wg_p), (Wu, wu_p), (Wd, wd_p))]
        for n, (src, dst, ex_) in enumerate(slabs):
            s, slot = n % NWB, 2 * n
            free = [S("vector", "wqkv_lo", k) for k in range(KD)] + [S("scalar", "wqkv_hi", k) for k in range(KD)]
            if n >= NWB:
                free = [S("gpsimd" if (n - NWB) % 2 else "vector", "slab_lo", n - NWB), S("scalar", "slab_hi", n - NWB)]
            raw = wb[:, s, :].rearrange("p (k n) -> p k n", k=KD)
            add("sync", slot, "load_slab", lambda e, b, raw=raw, src=src, ex_=ex_, s=s: e.dma_start(
                raw, src[ex_].rearrange("(k p) n -> p k n", p=P)).then_inc(dsem[f"slab{s}"], 16), *free)
            add("scalar", slot, ("slab_hi", n), lambda e, b, raw=raw, dst=dst, ex_=ex_: e.activation(
                dst[0][:, ex_, :, :], raw, ACT.Copy), ("once", f"slab{s}", n // NWB + 1, 0))
            add("gpsimd" if n % 2 else "vector", slot, ("slab_lo", n), lambda e, b, raw=raw, dst=dst, ex_=ex_: e.tensor_tensor(
                dst[1][:, ex_, :, :], raw, dst[0][:, ex_, :, :].bitcast(F32), ALU.subtract),
                S("scalar", "slab_hi", n))
        last_slabs = [S("gpsimd" if n % 2 else "vector", "slab_lo", n) for n in range(len(slabs) - 2, len(slabs))]

        def A(engine, *event):
            return at("att", engine, *event)

        def Ab(engine, *event):
            return before("att", engine, *event)

        def An(engine, *event):
            return ("att", engine, event, -1)

        def M(engine, *event):
            return at("moe", engine, *event)

        def Mb(engine, *event):
            return before("moe", engine, *event)

        add = att.add

        add("sync", 0, "load_x", lambda e, b: e.dma_start(
            xraw[:, :, :], xT[:, bass.ds(b, B)].rearrange("(k p) n -> p k n", p=P)).then_inc(dsem["x_raw"], 16),
            Ab("vector", "x1", KD - 1))
        add("sync", 0, "load_tab", lambda e, b: e.dma_start(
            tabs[:, :, :], tab[bass.ds(b, B), :].rearrange("(t p) n -> p t n", p=P)).then_inc(dsem["tab"], 16),
            Ab("vector", "cos", NT - 1), Ab("gpsimd", "sin1", NT - 1), Ab("gpsimd", "sin2", NT - 1))

        for k in range(KD):
            add("scalar", 0, ("x_hi", k), lambda e, b, k=k: e.activation(xo[0][:, k, :], xraw[:, k, :], ACT.Copy),
                dma("x_raw", 1, 1), Ab("tensor", "proj"))
            add("vector", 0, ("x_lo", k), lambda e, b, k=k: e.tensor_tensor(
                xo[1][:, k, :], xraw[:, k, :], xo[0][:, k, :].bitcast(F32), ALU.subtract), A("scalar", "x_hi", k))

        for t in range(NT):
            f = TILE[t]
            tok = slice(t * P, (t + 1) * P)
            s = t % 2
            add("sync", f, "load_xnat", lambda e, b, t=t, s=s: e.dma_start(
                xnat[:, s, :], x[bass.ds(b + t * P, P), :]).then_inc(dsem[f"x_nat{s}"], 16),
                (A if t >= 2 else Ab)("vector", "bn", t - 2 if t >= 2 else t + 2))
            add("vector", f, ("bn", t), lambda e, b, s=s: e.bn_stats(bst[:, :], xnat[:, s, :]),
                dma(f"x_nat{s}", 2, t // 2 + 1), (A if t else Ab)("vector", "mv", t - 1 if t else NT - 1))
            add("vector", f, ("mv", t), lambda e, b, t=t: (e.memset(idle[:, :], 0.0), e.bn_aggr(mv[:, t, :], bst[:, :]))[-1],
                A("vector", "bn", t), Ab("gpsimd", "rstd1", t))
            add("vector", f, ("ve", t), lambda e, b, t=t: e.tensor_scalar(
                ve[:, t:t + 1], mv[:, t, 1:2], EPS, None, ALU.add), A("vector", "mv", t))
            add("gpsimd", f, ("rstd1", t), lambda e, b, t=t: e.tensor_tensor(
                rstd1[:, t:t + 1], ve[:, t:t + 1], mhalf[:, 0:1], ALU.pow),
                A("vector", "ve", t), Ab("scalar", "qk", t), Ab("scalar", "v", t), S("vector", "mhalf"))

            def qkv(e, b, tok=tok):
                n = 0
                for k in range(KD):
                    for xi, wis in ((0, (0, 1)), (1, (0,))):
                        for wi in wis:
                            lhs = xo[xi][:, k, tok]
                            first, last = n == 0, n == 3 * KD - 1
                            e.matmul(R0[:, :], lhs, wqkv_p[wi][:, k, 0:2 * D], start=first, stop=last)
                            m = e.matmul(R1b[:, 0:D], lhs, wqkv_p[wi][:, k, 2 * D:], start=first, stop=last)
                            n += 1
                return m
            prev_t = (lambda eng, *ev: A(eng, *ev, t - 1)) if t else (lambda eng, *ev: Ab(eng, *ev, NT - 1))
            add("tensor", f, ("qkv", t), qkv, A("scalar", "x_hi", KD - 1), A("vector", "x_lo", KD - 1),
                prev_t("vector", "kT"), prev_t("vector", "qT1"), prev_t("scalar", "qT0"),
                S("vector", "wqkv_lo", KD - 1))

            add("scalar", f, ("qk", t), lambda e, b, t=t: e.activation(
                qk[:, :], R0[:, :], ACT.Copy, scale=rstd1[:, t:t + 1]),
                A("tensor", "qkv", t), A("gpsimd", "rstd1", t), prev_t("vector", "q_lo"), prev_t("gpsimd", "k_lo"))
            add("scalar", f, ("v", t), lambda e, b, t=t: e.activation(
                vs[:, :], R1b[:, 0:D], ACT.Copy, scale=rstd1[:, t:t + 1]),
                A("tensor", "qkv", t), A("gpsimd", "rstd1", t), prev_t("gpsimd", "v3"))

            qk_h = qk[:, :].rearrange("p (h s d) -> p h s d", s=2, d=HALF)
            r2_h = rop2[:, :].rearrange("p (h s d) -> p h s d", s=2, d=HALF)
            add("vector", f, ("cos", t), lambda e, b, t=t: e.tensor_tensor(
                rop[:, :].rearrange("p (h d) -> p h d", d=HALF), qk[:, :].rearrange("p (h d) -> p h d", d=HALF),
                bcast(tabs[:, t, 0:HALF], 1, 4 * H), ALU.mult),
                A("scalar", "qk", t), dma("tab", 1, 1), prev_t("scalar", "relu"), prev_t("scalar", "exp"))
            for s2, at_ in ((0, HALF), (1, 2 * HALF)):
                add("gpsimd", f, ("sin" + str(s2 + 1), t), lambda e, b, t=t, s2=s2, at_=at_: e.tensor_tensor(
                    r2_h[:, :, s2, :], qk_h[:, :, 1 - s2, :], bcast(tabs[:, t, at_:at_ + HALF], 1, 2 * H), ALU.mult),
                    A("scalar", "qk", t), dma("tab", 1, 1), prev_t("vector", "phi"))
            add("vector", f, ("rope", t), lambda e, b: e.tensor_tensor(rop[:, :], rop[:, :], rop2[:, :], ALU.add),
                A("vector", "cos", t), A("gpsimd", "sin1", t), A("gpsimd", "sin2", t))
            add("scalar", f, ("exp", t), lambda e, b: e.activation(ex[:, :], rop[:, :], ACT.Exp),
                A("vector", "rope", t), prev_t("vector", "phi"))
            add("scalar", f, ("relu", t), lambda e, b: e.activation(rop2[:, :], rop[:, :], ACT.Relu),
                A("vector", "rope", t))
            add("vector", f, ("phi", t), lambda e, b: e.scalar_tensor_tensor(
                out=qk[:, :], in0=ex[:, :], scalar=1.0, in1=rop2[:, :], op0=ALU.min, op1=ALU.add),
                A("scalar", "exp", t), A("scalar", "relu", t), A("gpsimd", "sin2", t), A("vector", "cos", t))
            f_q = bcast(qk[:, 0:D].rearrange("p (h d) -> p h d", d=HD), 2, 2)
            f_k = bcast(qk[:, D:].rearrange("p (h d) -> p h d", d=HD), 2, 2)
            add("scalar", f, ("q_hi", t), lambda e, b, f_q=f_q: e.activation(stack[:, 0:H, 0:2, :], f_q, ACT.Copy),
                A("vector", "phi", t), prev_t("tensor", "state"))
            add("scalar", f, ("k_hi", t), lambda e, b, f_k=f_k: e.activation(stack[:, H:, 0::2, :], f_k, ACT.Copy),
                A("vector", "phi", t), prev_t("tensor", "state"))
            add("vector", f, ("q_lo", t), lambda e, b, f_q=f_q: e.tensor_tensor(
                stack[:, 0:H, 2:4, :], f_q, stack[:, 0:H, 0:2, :], ALU.subtract), A("scalar", "q_hi", t))
            add("gpsimd", f, ("k_lo", t), lambda e, b, f_k=f_k: e.tensor_tensor(
                stack[:, H:, 1::2, :], f_k, stack[:, H:, 0::2, :], ALU.subtract), A("scalar", "k_hi", t))
            v_h = vs[:, :].rearrange("p (h d) -> p h d", d=HD)
            add("scalar", f, ("v1", t), lambda e, b: e.activation(vx[:, :, 0, 0:HD], v_h, ACT.Copy),
                A("scalar", "v", t), prev_t("tensor", "state"), S("vector", "z_vx"))
            add("gpsimd", f, ("vr", t), lambda e, b: e.tensor_tensor(v_h, v_h, vx[:, :, 0, 0:HD], ALU.subtract),
                A("scalar", "v1", t))
            add("scalar", f, ("v2", t), lambda e, b: e.activation(vx[:, :, 1, 0:HD], v_h, ACT.Copy),
                A("gpsimd", "vr", t))
            add("gpsimd", f, ("v3", t), lambda e, b: e.tensor_tensor(
                vx[:, :, 2, 0:HD], v_h, vx[:, :, 1, 0:HD], ALU.subtract), A("scalar", "v2", t))

            kTp, qTp = (r[:, :].bitcast(F16).rearrange("p (a b) -> p a b", a=NP) for r in (R0, R1b))

            def turn(e, b, dst, first):
                for p in range(NP):
                    m = e.transpose(dst[:, p, :], stack[:, first + 2 * p:first + 2 * p + 2, :, :]
                                    .rearrange("p h c d -> p (h c d)"), ident16[:, :])
                return m
            add("tensor", f, ("k_T", t), lambda e, b, d=kTp: turn(e, b, d, H),
                A("scalar", "k_hi", t), A("gpsimd", "k_lo", t), A("scalar", "qk", t), S("vector", "id16"),
                *((Ab("scalar", "wt"),) if t == 1 else ()))
            add("tensor", f, ("q_T", t), lambda e, b, d=qTp: turn(e, b, d, 0),
                A("scalar", "q_hi", t), A("vector", "q_lo", t), A("scalar", "v", t), S("vector", "id16"))
            add("vector", f, ("kT", t), lambda e, b, s_=kTp: e.tensor_copy(kT[:, :, :], s_),
                A("tensor", "k_T", t), *[prev_t("tensor", f"qk{r}") for r in range(4)])
            add("scalar", f, ("qT0", t), lambda e, b, s_=qTp: e.activation(qbd[0:64, :, 0, :], s_[0:64], ACT.Copy),
                A("tensor", "q_T", t), prev_t("tensor", "av0"), prev_t("tensor", "av1"), S("vector", "z_qbd"))
            add("vector", f, ("qT1", t), lambda e, b, s_=qTp: e.tensor_copy(qbd[64:P, :, 1, :], s_[64:P]),
                A("tensor", "q_T", t), prev_t("tensor", "av0"), prev_t("tensor", "av1"), S("vector", "z_qbd"))

            for r in range(4):
                bank = BK[r % 2]
                if r >= 2:
                    free = (A("vector", f"mask{r - 2}", t),)
                elif t:
                    free = tuple(A("vector", f"st{r}_{hh}", t - 1) for hh in range(2)) + (
                        (A("vector", "o_lo", t - 1),) if r else ())
                else:
                    free = (Ab("vector", "ln2", KD - 1),) if r else (Ab("vector", "router", "z"),)
                add("tensor", f, (f"qk{r}", t), lambda e, b, r=r, bank=bank: [e.matmul(
                    bank[:, 2 * P * j:2 * P * (j + 1)], kT[:, 2 * r + j, :],
                    qbd[:, 2 * r + j, :, :].rearrange("p a b -> p (a b)"), start=True, stop=True)
                    for j in range(2)][-1],
                    A("vector", "kT", t), A("vector", "qT1", t), A("scalar", "qT0", t), *free)
                add("vector", f, (f"mask{r}", t), lambda e, b, r=r, bank=bank: e.tensor_tensor(
                    am[:, r % 2, :].rearrange("p (h n) -> p h n", h=4), bank[:, :].rearrange("p (h n) -> p h n", h=4),
                    bcast(cmask[:, :], 1, 4), ALU.mult),
                    A("tensor", f"qk{r}", t), S("gpsimd", "mask"),
                    A("gpsimd", f"a_lo{r - 2}", t) if r >= 2 else prev_t("gpsimd", f"a_lo{r + 2}"))
                a4 = am[:, r % 2, :].rearrange("p (h n) -> p h n", h=4)
                add("scalar", f, (f"a_hi{r}", t), lambda e, b, r=r, a4=a4: e.activation(
                    a_p[0][:, 4 * r:4 * r + 4, :], a4, ACT.Copy),
                    A("vector", f"mask{r}", t), prev_t("tensor", f"av{r // 2}"))
                add("gpsimd", f, (f"a_lo{r}", t), lambda e, b, r=r, a4=a4: e.tensor_tensor(
                    a_p[1][:, 4 * r:4 * r + 4, :], a4, a_p[0][:, 4 * r:4 * r + 4, :], ALU.subtract),
                    A("scalar", f"a_hi{r}", t))

            def attend(e, b, g):
                for h in range(8 * g, 8 * g + 8):
                    o = BK[g][:, (h % 8) * WV:(h % 8 + 1) * WV]
                    e.matmul(o, qbd[:, h // 2, h % 2, :], st_x[:, h // 2, :, :].rearrange("p a b -> p (a b)"),
                             start=(h % 8 == 0), stop=False, skip_group_check=True)
                for h in range(8 * g, 8 * g + 8):
                    o = BK[g][:, (h % 8) * WV:(h % 8 + 1) * WV]
                    for a in a_p:
                        m = e.matmul(o, a[:, h, :], vx[:, h, :, :].rearrange("p a b -> p (a b)"),
                                     start=False, stop=(h % 8 == 7), skip_group_check=True)
                return m
            for g in range(2):
                add("tensor", f, (f"av{g}", t), lambda e, b, g=g: attend(e, b, g),
                    A("vector", f"mask{2 + g}", t), A("gpsimd", f"a_lo{2 * g}", t), A("scalar", f"a_hi{2 * g}", t),
                    A("gpsimd", f"a_lo{2 * g + 1}", t), A("scalar", f"a_hi{2 * g + 1}", t),
                    A("gpsimd", "v3", t), A("scalar", "v2", t),
                    prev_t("gpsimd", "s3"), prev_t("scalar", "s2"), S("vector", "z_sx"), S("vector", "one_vx"))
                add("vector", f, (f"o{g}", t), lambda e, b, g=g: e.tensor_reduce(
                    osb[:, 8 * g:8 * g + 8, :],
                    BK[g][:, 0:8 * WV].rearrange("p (h s d) -> p h d s", s=3, d=W1), AX.X, ALU.add),
                    A("tensor", f"av{g}", t), prev_t("vector", "norm"))

            def state(e, b):
                for p in range(NP):
                    m = e.matmul(BK[p // 4][:, (p % 4) * 2 * WV:(p % 4 + 1) * 2 * WV],
                                 stack[:, H + 2 * p:H + 2 * p + 2, :, :].rearrange("p h c d -> p (h c d)"),
                                 vx[:, 2 * p:2 * p + 2, :, :].rearrange("p h a b -> p (h a b)"),
                                 start=(p % 4 == 0), stop=(p % 4 == 3), skip_group_check=True)
                return m
            add("tensor", f, ("state", t), state, A("vector", "o0", t), A("vector", "o1", t))
            for g in range(2):
                for hh in range(2):
                    rows = slice(64 * hh, 64 * hh + 64)
                    add("vector", f, (f"st{g}_{hh}", t),
                        lambda e, b, g=g, hh=hh, rows=rows: e.tensor_reduce(
                            st_d[rows, 4 * g:4 * g + 4, :],
                            BK[g][rows, 0:8 * WV].rearrange("p (q h s d) -> p q h d s", h=2, s=3, d=W1)[:, :, hh, :, :],
                            AX.X, ALU.add), A("tensor", "state", t), prev_t("vector", "ss"))
            add("vector", f, ("ss", t), lambda e, b: e.scalar_tensor_tensor(
                out=st_s[:, :, :], in0=st_d[:, :, :], scalar=ASCALE, in1=st_s[:, :, :], op0=ALU.mult, op1=ALU.add),
                A("vector", "st1_1", t), A("vector", "st0_0", t), A("vector", "st0_1", t), A("vector", "st1_0", t),
                prev_t("gpsimd", "sr"), prev_t("scalar", "s1"), S("vector", "z_ss"))
            add("scalar", f, ("s1", t), lambda e, b: e.activation(st_x[:, :, 0, :], st_s[:, :, :], ACT.Copy),
                A("vector", "ss", t), A("tensor", "av0", t), A("tensor", "av1", t), S("vector", "z_sx"))
            add("gpsimd", f, ("sr", t), lambda e, b: e.tensor_tensor(
                st_r[:, :, :], st_s[:, :, :], st_x[:, :, 0, :], ALU.subtract), A("scalar", "s1", t),
                prev_t("gpsimd", "s3"))
            add("scalar", f, ("s2", t), lambda e, b: e.activation(st_x[:, :, 1, :], st_r[:, :, :], ACT.Copy),
                A("gpsimd", "sr", t))
            add("gpsimd", f, ("s3", t), lambda e, b: e.tensor_tensor(
                st_x[:, :, 2, :], st_r[:, :, :], st_x[:, :, 1, :], ALU.subtract), A("scalar", "s2", t))

            add("vector", f, ("den", t), lambda e, b: e.tensor_scalar(
                den[:, :], osb[:, :, HD], 1.0 / ASCALE, 1e-6, ALU.mult, ALU.max),
                A("vector", "o0", t), A("vector", "o1", t), prev_t("vector", "rec"))
            add("vector", f, ("rec", t), lambda e, b: e.reciprocal(rec[:, :], den[:, :]), A("vector", "den", t))
            add("vector", f, ("norm", t), lambda e, b: e.scalar_tensor_tensor(
                out=onrm[:, :].rearrange("p (h d) -> p h d", d=HD), in0=osb[:, :, 0:HD], scalar=1.0 / ASCALE,
                in1=bcast(rec[:, :], 2, HD), op0=ALU.mult, op1=ALU.mult),
                A("vector", "rec", t), prev_t("tensor", "o_T"))
            add("tensor", f, ("o_T", t), lambda e, b: [e.transpose(
                R3[:, k * P:(k + 1) * P], onrm[:, k * P:(k + 1) * P], ident[:, :]) for k in range(KD)][-1],
                A("vector", "norm", t), A("vector", "st1_0", t), A("vector", "st1_1", t), S("gpsimd", "id"))
            oT = R3[:, 0:D].rearrange("p (k n) -> p k n", k=KD)
            add("scalar", f, ("o_hi", t), lambda e, b, tok=tok, oT=oT: e.activation(xo[0][:, :, tok], oT, ACT.Copy),
                A("tensor", "o_T", t))
            add("vector", f, ("o_lo", t), lambda e, b, tok=tok, oT=oT: e.tensor_tensor(
                xo[1][:, :, tok], oT, xo[0][:, :, tok].bitcast(F32), ALU.subtract), A("scalar", "o_hi", t))

        z = Z0

        def proj(e, b):
            for m_ in range(KD):
                n = 0
                for k in range(KD):
                    for wi, xi in ((0, 0), (1, 0), (0, 1)):
                        mm = e.matmul(BK[m_][:, :], wout_p[wi][:, k, m_ * P:(m_ + 1) * P], xo[xi][:, k, :],
                                      start=(n == 0), stop=(n == 3 * KD - 1))
                        n += 1
            return mm
        add("tensor", z, ("proj",), proj, A("scalar", "o_hi", NT - 1), A("vector", "o_lo", NT - 1),
            A("vector", "st0_0", NT - 1), A("vector", "st0_1", NT - 1),
            S("vector", "wout_lo"))
        for k in range(KD):
            add("vector", z, ("x1", k), lambda e, b, k=k: e.tensor_tensor(x1[:, k, :], BK[k][:, :], xraw[:, k, :], ALU.add),
                A("tensor", "proj"), Ab("scalar", "x2_hi", k), Ab("vector", "x2_lo", k))
        add("sync", z, "store_x1", lambda e, b: e.dma_start(x1_scr.rearrange("(k p) n -> p k n", p=P), x1[:, :, :])
            .then_inc(dsem["x1_out"], 16), A("vector", "x1", KD - 1), dma("x1_in", 1, 1, 1))
        add("tensor", z, ("mean2",), lambda e, b: [e.matmul(
            R2[:, :], mean_w[:, :], x1[:, k, :], start=(k == 0), stop=(k == KD - 1)) for k in range(KD)][-1],
            A("vector", "x1", 0), A("vector", "x1", 1))
        for k in range(KD):
            add("vector", z, ("xc", k), lambda e, b, k=k: e.tensor_tensor(
                x1[:, k, :], x1[:, k, :], R2[:, :], ALU.subtract), A("tensor", "mean2"), dma("x1_out", 1, 1))
            add("scalar", z, ("sq", k), lambda e, b, k=k: e.activation(sq[:, :], x1[:, k, :], ACT.Square),
                A("vector", "xc", k), A("tensor", "var2", k - 1) if k else Ab("tensor", "var2", KD - 1))
            add("tensor", z + k, ("var2", k), lambda e, b, k=k: [e.matmul(
                R3[:, t:t + 1], sq[:, t * P:(t + 1) * P], mean_w[:, 0:1], start=(k == 0 and t == 0),
                stop=(k == KD - 1 and t == NT - 1), skip_group_check=True) for t in range(NT)][-1],
                A("scalar", "sq", k), A("vector", "x1", 1))
        add("tensor", z, ("logit",), lambda e, b: [e.matmul(
            R2[:, t * E:(t + 1) * E], x1[:, k, t * P:(t + 1) * P], wr_sb[:, k, :], start=(k == 0 and t == 0),
            stop=(k == KD - 1 and t == NT - 1), skip_group_check=True) for k in range(KD) for t in range(NT)][-1],
            A("vector", "xc", 0), A("vector", "xc", 1), ("once", "c_wr", 1, 0))
        add("vector", z, ("v2n",), lambda e, b: e.tensor_scalar(v2n[:, :], R3[:, 0:NT], EPS, None, ALU.add),
            A("tensor", "var2", KD - 1))
        add("gpsimd", z, ("r2n",), lambda e, b: e.tensor_tensor(r2n[:, :], v2n[:, :], mhalf[:, :], ALU.pow),
            A("vector", "v2n"))
        add("tensor", z, ("rstd2",), lambda e, b: [e.transpose(
            R3[:, t * P:(t + 1) * P], r2n[:, t:t + 1].broadcast_to([P, P]), ident[:, :]) for t in range(NT)][-1],
            A("gpsimd", "r2n"))
        for k in range(KD):
            add("vector", z, ("ln2", k), lambda e, b, k=k: e.tensor_tensor(
                x1[:, k, :], x1[:, k, :], R3[:, :], ALU.mult), A("tensor", "rstd2"), A("tensor", "logit"))

        r_ = {n: v[:, :, :] for n, v in R.items()}
        q_ = {n: v[:, :] for n, v in R1.items()}
        lg = R2[:, 0:NT * E].rearrange("p (t n) -> p t n", n=E)
        io = bcast(iota[:, :], 1, NT)
        V = "vector"
        steps = [
            (V, "z", lambda e: e.tensor_tensor(r_["z"], lg, bcast(r2n[:, :], 2, E), ALU.mult), ()),
            ("scalar", "th", lambda e: e.activation(r_["th"], r_["z"], ACT.Tanh, scale=rtemp[:, 0:1]), ("z",)),
            (V, "inh", lambda e: e.tensor_scalar(r_["inh"], r_["th"], 0.5, 0.5, ALU.mult, ALU.add), ("th",)),
            (V, "off", lambda e: e.tensor_scalar(r_["nd"], r_["inh"], G_CENTER, None, ALU.subtract), ("inh",)),
            (V, "zone", lambda e: e.tensor_scalar(r_["zone"], r_["inh"], G_LOWER, None, ALU.is_ge), ("inh",)),
            (V, "dist", lambda e: e.scalar_tensor_tensor(
                out=r_["dist"], in0=r_["nd"], scalar=-1.0, in1=r_["nd"], op0=ALU.mult, op1=ALU.max), ("off",)),
            ("scalar", "e1", lambda e: e.activation(r_["e1"], r_["dist"], ACT.Exp, scale=-1.0 / 0.1), ("dist",)),
            ("scalar", "fb", lambda e: e.activation(r_["fb"], r_["dist"], ACT.Exp, scale=-1.0 / 0.3), ("dist",)),
            (V, "zone2", lambda e: e.scalar_tensor_tensor(
                out=r_["zone2"], in0=r_["inh"], scalar=G_UPPER, in1=r_["zone"], op0=ALU.is_le, op1=ALU.mult), ("zone",)),
            (V, "m", lambda e: e.tensor_reduce(q_["m"], r_["dist"], AX.X, ALU.min), ("dist",)),
            (V, "eq", lambda e: e.tensor_tensor(r_["eq"], r_["dist"], bcast(q_["m"], 2, E), ALU.not_equal), ("m",)),
            (V, "w0", lambda e: e.tensor_tensor(r_["w0"], r_["e1"], r_["zone2"], ALU.mult), ("e1", "zone2")),
            (V, "c", lambda e: e.scalar_tensor_tensor(
                out=r_["c"], in0=r_["eq"], scalar=99.0, in1=io, op0=ALU.mult, op1=ALU.add), ("eq",)),
            (V, "ws", lambda e: e.tensor_reduce(q_["ws"], r_["w0"], AX.X, ALU.add), ("w0",)),
            (V, "ix", lambda e: e.tensor_reduce(q_["ix"], r_["c"], AX.X, ALU.min), ("c",)),
            (V, "no", lambda e: e.tensor_scalar(q_["no"], q_["ws"], 1e-8, None, ALU.is_lt), ("ws",)),
            (V, "s1", lambda e: e.tensor_tensor(r_["s1"], io, bcast(q_["ix"], 2, E), ALU.is_equal), ("ix",)),
            (V, "yes", lambda e: e.tensor_scalar(q_["yes"], q_["ws"], 1e-8, None, ALU.is_ge), ("ws",)),
            (V, "nd", lambda e: e.scalar_tensor_tensor(
                out=r_["nd"], in0=r_["s1"], scalar=9.0, in1=r_["dist"], op0=ALU.mult, op1=ALU.add), ("s1",)),
            (V, "w1", lambda e: e.tensor_tensor(r_["w0"], r_["w0"], bcast(q_["yes"], 2, E), ALU.mult), ("yes",)),
            (V, "m2", lambda e: e.tensor_reduce(q_["m2"], r_["nd"], AX.X, ALU.min), ("nd",)),
            (V, "fbn", lambda e: e.tensor_tensor(r_["fw"], r_["fb"], bcast(q_["no"], 2, E), ALU.mult), ("fb", "no")),
            (V, "eq2", lambda e: e.tensor_tensor(r_["eq"], r_["nd"], bcast(q_["m2"], 2, E), ALU.not_equal), ("m2", "c")),
            (V, "c2", lambda e: e.scalar_tensor_tensor(
                out=r_["c"], in0=r_["eq"], scalar=99.0, in1=io, op0=ALU.mult, op1=ALU.add), ("eq2",)),
            (V, "ix2", lambda e: e.tensor_reduce(q_["ix2"], r_["c"], AX.X, ALU.min), ("c2",)),
            (V, "s2", lambda e: e.tensor_tensor(r_["s2"], io, bcast(q_["ix2"], 2, E), ALU.is_equal), ("ix2",)),
            (V, "s12", lambda e: e.tensor_tensor(r_["s1"], r_["s1"], r_["s2"], ALU.add), ("s2",)),
            (V, "fw", lambda e: e.tensor_tensor(r_["fw"], r_["fw"], r_["s1"], ALU.mult), ("s12", "fbn")),
            (V, "w", lambda e: e.tensor_tensor(r_["w"], r_["w0"], r_["fw"], ALU.add), ("fw", "w1")),
            (V, "w2", lambda e: e.tensor_reduce(q_["w2"], r_["w"], AX.X, ALU.add), ("w",)),
            (V, "w3", lambda e: e.tensor_scalar(q_["w2"], q_["w2"], 1e-8, 2.0, ALU.max, ALU.mult), ("w2",)),
            (V, "w4", lambda e: e.reciprocal(q_["w2"], q_["w2"]), ("w3",)),
            (V, "wo", lambda e: e.tensor_tensor(r_["wo"], r_["w"], bcast(q_["w2"], 2, E), ALU.mult), ("w4",)),
        ]
        made_by = {name: eng for eng, name, _, _ in steps}
        for n, (eng, name, fn, needs) in enumerate(steps):
            waits = [A(made_by[need], "router", need) for need in needs]
            if name == "z":
                waits += [A("tensor", "logit"), A("gpsimd", "r2n")]
            if name == "th":
                waits += [S("vector", "rtemp2")]
            if name == "inh":
                waits += [Ab("tensor", "w_T"), S("vector", "iota")]
            add(eng, z + n * 0.13, ("router", name), lambda e, b, fn=fn: fn(e), *waits)
        add("tensor", z, ("w_T",), lambda e, b: [e.transpose(
            R0[0:E, t * P:(t + 1) * P], R["wo"][:, t, :], ident[:, :]) for t in range(NT)][-1],
            A("vector", "router", "wo"), An("scalar", "qk", 1))
        add("scalar", z, ("wt",), lambda e, b: e.activation(rt[:, :], R0[0:E, :], ACT.Copy), A("tensor", "w_T"),
            dma("w_out", 1, 1, 1))
        add("scalar", z, "store_w", lambda e, b: e.dma_start(w_scr, rt[:, :]).then_inc(dsem["w_out"], 16),
            A("scalar", "wt"), *[dma(f"wb{i}", len(range(i, E, NWB)), len(range(i, E, NWB)), 1) for i in range(NWB)])

        for k in range(KD):
            att.add("scalar", M0, ("x2_hi", k), lambda e, b, k=k: e.activation(x2[0][:, k, :], x1[:, k, :], ACT.Copy),
                A("vector", "ln2", k), Mb("tensor", "gate", UNITS - 1), Mb("tensor", "up", UNITS - 1))
            att.add("vector", M0, ("x2_lo", k), lambda e, b, k=k: e.tensor_tensor(
                x2[1][:, k, :], x1[:, k, :], x2[0][:, k, :].bitcast(F32), ALU.subtract), A("scalar", "x2_hi", k))

        add = moe.add
        add("sync", M0, "load_x1", lambda e, b: e.dma_start(x1r[:, :, :], x1_scr.rearrange("(k p) n -> p k n", p=P))
            .then_inc(dsem["x1_in"], 16), dma("x1_out", 1, 1), dma("y_out", 1, 1, 1), S("vector", "wout_lo"))
        for e_ in range(E):
            s, n = e_ % NWB, e_ // NWB + 1
            cnt = len(range(s, E, NWB))
            if e_ < NWB:
                last_use = max(x_ for x_ in range(E) if x_ % NWB == s)
                free = [Mb("vector", "gw", 2 * last_use + 1)] + last_slabs
            else:
                free = [M("vector", "gw", 2 * (e_ - NWB) + 1)]
            add("sync", M0 + max(0, 6 * (e_ - NWB) + 8), "load_w", lambda e, b, e_=e_, s=s: e.dma_start(
                wb[:, s, :], w_scr[e_:e_ + 1, :].broadcast_to([P, B])).then_inc(dsem[f"wb{s}"], 16),
                dma("w_out", 1, 1), *free)

        def three(e, out, w, wsel, xs, xsel, start, stop):
            todo = [(wi, xi, k) for wi, xi in ((0, 0), (1, 0), (0, 1)) for k in range(len(wsel))]
            for n, (wi, xi, k) in enumerate(todo):
                m = e.matmul(out, wsel[k](w[wi]), xsel[k](xs[xi]), start=start and n == 0,
                             stop=stop and n == len(todo) - 1, skip_group_check=not (start and stop))
            return m

        for u in range(UNITS):
            e_, m_ = u // KI, u % KI
            c = slice(m_ * P, (m_ + 1) * P)
            hs = u % 2
            prv = (lambda eng, ev, d=1: M(eng, ev, u - d) if u >= d else Mb(eng, ev, UNITS + u - d))
            wsel = [lambda w, k=k, e_=e_, c=c: w[:, e_, k, c] for k in range(KD)]
            xsel = [lambda x_, k=k: x_[:, k, :] for k in range(KD)]
            add("tensor", M0 + 3 * u, ("gate", u), lambda e, b, wsel=wsel, xsel=xsel: three(
                e, G[:, :], wg_p, wsel, x2, xsel, True, True),
                prv("vector", "g"), A("scalar", "x2_hi", KD - 1), A("vector", "x2_lo", KD - 1), *last_slabs)
            add("tensor", M0 + 3 * u, ("up", u), lambda e, b, wsel=wsel, xsel=xsel: three(
                e, U[:, :], wu_p, wsel, x2, xsel, True, True), prv("vector", "h"),
                A("scalar", "x2_hi", KD - 1), A("vector", "x2_lo", KD - 1), *last_slabs)
            add("scalar", M0 + 3 * u, ("tanh", u), lambda e, b, hs=hs: e.activation(hb[:, hs, :], G[:, :], ACT.Tanh, scale=0.5),
                M("tensor", "gate", u), prv("gpsimd", "h_lo", 2), prv("scalar", "h_hi", 2))
            add("vector", M0 + 3 * u, ("g", u), lambda e, b, hs=hs: e.scalar_tensor_tensor(
                out=hb[:, hs, :], in0=hb[:, hs, :], scalar=1.0, in1=G[:, :], op0=ALU.add, op1=ALU.mult),
                M("scalar", "tanh", u))
            add("vector", M0 + 3 * u, ("h", u), lambda e, b, hs=hs: e.tensor_tensor(
                hb[:, hs, :], hb[:, hs, :], U[:, :], ALU.mult), M("vector", "g", u), M("tensor", "up", u))
            add("vector", M0 + 3 * u, ("gw", u), lambda e, b, hs=hs, e_=e_: e.tensor_tensor(
                hb[:, hs, :], hb[:, hs, :], wb[:, e_ % NWB, :], ALU.mult),
                M("vector", "h", u), dma(f"wb{e_ % NWB}", len(range(e_ % NWB, E, NWB)), e_ // NWB + 1))
            add("scalar", M0 + 3 * u, ("h_hi", u), lambda e, b, hs=hs: e.activation(h_p[0][:, hs, :], hb[:, hs, :], ACT.Copy),
                M("vector", "gw", u), prv("tensor", "down", 2))
            add("gpsimd", M0 + 3 * u, ("h_lo", u), lambda e, b, hs=hs: e.tensor_tensor(
                h_p[1][:, hs, :], hb[:, hs, :], h_p[0][:, hs, :].bitcast(F32), ALU.subtract),
                M("scalar", "h_hi", u), prv("tensor", "down", 2))

            def down(e, b, u=u, e_=e_, m_=m_, hs=hs):
                for wi, hi in ((0, 0), (1, 0), (0, 1)):
                    for d in range(KD):
                        mm = e.matmul(Y[d][:, :], wd_p[wi][:, e_, m_, d * P:(d + 1) * P], h_p[hi][:, hs, :],
                                      start=(u == 0 and (wi, hi) == (0, 0)),
                                      stop=(u == UNITS - 1 and hi == 1), skip_group_check=True)
                return mm
            waits = [M("scalar", "h_hi", u), M("gpsimd", "h_lo", u), *last_slabs]
            if u == 0:
                waits += [Mb("vector", "y", k) for k in range(KD)]
            add("tensor", M0 + 3 * u, ("down", u), down, *waits)
        for k in range(KD):
            add("vector", M0 + SLOTS, ("y", k), lambda e, b, k=k: e.tensor_tensor(
                x1r[:, k, :], Y[k][:, :], x1r[:, k, :], ALU.add), M("tensor", "down", UNITS - 1), dma("x1_in", 1, 1))
        add("scalar", M0 + SLOTS, "store_y", lambda e, b: e.dma_start(
            outT[:, bass.ds(b, B)].rearrange("(k p) n -> p k n", p=P), x1r[:, :, :]).then_inc(dsem["y_out"], 16),
            M("vector", "y", KD - 1))

        for part in parts.values():
            part.close()
        LATE = max(late for part in parts.values() for late, _ in part.count)
        sems = {(part.name, late, e): sem(f"{part.name}{late}_{e}")
                for part in parts.values() for late, e in part.count}

        def emit(engine, eng, stage, first, last):
            merged = []
            for n, (name, part) in enumerate(parts.items()):
                for slot, late, event, fn, waits in part.ops[engine]:
                    if (name == "setup" and first == 0) or (name != "setup" and 0 <= first - late and last - late < NB):
                        merged.append((slot - late * SLOTS, n, name, late, event, fn, waits))
            merged.sort(key=lambda x_: x_[:2])
            seen = {}
            rows = {late: (stage - late) * B if isinstance(stage, int) else eng.snap((stage - late) * B)
                    for late in range(LATE + 1)} if engine in ("sync", "scalar") else {}
            for _, _, name, late, event, fn, waits in merged:
                b = stage - late if name != "setup" else 0
                todo = []
                for kind, producer, w_event, back in waits:
                    if isinstance(b, int) and b - back >= NB:
                        continue
                    if kind == "once":
                        sm, per, rel = dsem[producer], 0, 16 * w_event
                    elif kind == "dma":
                        (n, k) = w_event
                        sm, per, rel = dsem[producer], 16 * n, 16 * (k + ((producer == "y_out") - back) * n)
                    else:
                        its, number = parts[kind].number[producer, w_event]
                        n = parts[kind].count[its, producer] if kind != "setup" else 0
                        sm, per = sems[kind, its, producer], n
                        rel = number + (1 - back) * n
                    value = b * per + rel
                    if isinstance(value, int):
                        if value <= 0:
                            continue
                        key, known = sm.name, value
                    else:
                        key, known = (sm.name, late, per == 0), rel
                    if seen.get(key, 0) < known or key not in seen:
                        seen[key] = known
                        todo.append((sm, value))
                for n, (sm, value) in enumerate(todo):
                    eng.wait_ge(sm, value)
                    if engine == "sync" and not isinstance(b, int):
                        eng.sem_inc(carrier, 1)
                ins = fn(eng, rows[late] if isinstance(event, str) else b)
                if isinstance(event, tuple):
                    ins.then_inc(sems[name, late, engine], 1)

        def program(engine):
            def run(eng):
                for (name, late, owner), sm in sems.items():
                    if owner == engine and name != "setup":
                        eng.sem_inc(sm, parts[name].count[late, owner])
                if engine == "sync":
                    eng.sem_inc(dsem["y_out"], 16)
                for stage in range(LATE):
                    emit(engine, eng, stage, stage, stage)
                with eng.Fori(LATE, NB) as i:
                    emit(engine, eng, i, LATE, NB - 1)
                for stage in range(NB, NB + LATE):
                    emit(engine, eng, stage, stage, stage)
                if engine == "sync":
                    for n in ("x1_out", "w_out", "y_out"):
                        eng.wait_ge(dsem[n], 16 * (NB + (n == "y_out")))
            return run

        block = ctx.enter_context(nc.Block())
        block.tensor(program("tensor"))
        block.scalar(program("scalar"))
        block.vector(program("vector"))
        block.gpsimd(program("gpsimd"))
        block.sync(program("sync"))


def kernel(**inputs):
    import concourse.bacc as bacc
    from concourse.bass_utils import run_bass_kernel_spmd

    x = np.asarray(inputs["L0_attn_x"])
    inv_freq = (np.float32(1.0) / np.power(np.float32(10000.0), np.arange(HALF, dtype=np.float32) / np.float32(HALF)))
    ang = (np.arange(N, dtype=np.float32)[:, None] * inv_freq.astype(np.float32)[None, :]).astype(np.float64)
    cos, sin = (f(ang).astype(np.float32) * np.float32(SCALE) for f in (np.cos, np.sin))
    arrays = {
        "x": np.ascontiguousarray(x[0]),
        "xT": np.ascontiguousarray(x[0].T),
        "w_qkv": np.ascontiguousarray(inputs["L0_attn_w_qkv"]),
        "w_out": np.ascontiguousarray(inputs["L0_attn_w_out"]),
        "Wg": np.ascontiguousarray(inputs["L0_ffn_Wg"]),
        "Wu": np.ascontiguousarray(inputs["L0_ffn_Wu"]),
        "Wd": np.ascontiguousarray(inputs["L0_ffn_Wd"]),
        "Wr": np.ascontiguousarray(inputs["L0_ffn_Wr"]),
        "temperature": np.ascontiguousarray(inputs["L0_ffn_temperature"]),
        "tab": np.concatenate([cos, -sin, sin], axis=1),
    }
    nc = bacc.Bacc("TRN2", target_bir_lowering=False, num_devices=1)
    args = [nc.dram_tensor(n, list(a.shape), F32, kind="ExternalInput").ap() for n, a in arrays.items()]
    args.append(nc.dram_tensor("outT", [D, N], F32, kind="ExternalOutput").ap())
    args.append(nc.dram_tensor("w_scr", [E, B], F32, kind="Internal").ap())
    args.append(nc.dram_tensor("x1_scr", [D, B], F32, kind="Internal").ap())
    build(nc, *args)
    r = run_bass_kernel_spmd(nc, [arrays], core_ids=[0])
    return np.ascontiguousarray(r.results[0]["outT"].T)[None]
```

```python
from contextlib import ExitStack

import numpy as np

import concourse.bass as bass
from concourse import mybir

F32 = mybir.dt.float32
F32R = mybir.dt.float32r
F16 = mybir.dt.float16
BF16 = mybir.dt.bfloat16
ALU = mybir.AluOpType
ACT = mybir.ActivationFunctionType
AX = mybir.AxisListType

P = 128
N, D = 4096, 256
B = 512
NB = N // B
NT = B // P
KD = D // P
H, HD = 16, 16
HALF = HD // 2
NP = H // 2
E, I = 8, 256
KI = I // P
UNITS = E * KI
W1 = HD + 1
WV = 3 * W1
SCALE = float(HD ** -0.25)
EPS = 1e-5
ASCALE = 1.0 / 16.0
G_CENTER = 1.0 / float(np.e)
G_LOWER = 0.5 - float(np.log(4.0 / 3.0))
G_UPPER = 0.5
SLOTS = 3 * UNITS
TILE = (4, 13, 22, 31)
Z0 = 52
M0 = 66
SLABS_WB, SLAB_STEP = 12, 3
NWB = 3
PLACE = {
    "setup": {
        "load_w_qkv": 0, "load_w_out": 0, "load_Wr": 0, "load_temperature": 0, "ones": 0, "mhalf": 0,
        "rtemp": 3.5, "rtemp2": 42.75, "id0": 0, "mask0": 0, "id": 0, "mask": 0, "iota_i": 0, "iota": 0,
        "id16": 0, "z_qbd": 0, "z_vx": 0, "one_vx": 16.5, "z_sx": 16.75, "z_ss": 0, "colmean": 0, "wc": 5.75,
        "wqkv_hi": 5.75, "wqkv_lo": 6, "wout_hi": 1, "wout_lo": 2, "load_slab": 24.25, "slab_hi": 11,
        "slab_lo": 12,
    },
    "att": {
        "load_x": 15.75, "load_tab": 9.5, "x_hi": 5, "x_lo": 2, "load_xnat": -4, "bn": -3.5, "mv": -3, "ve": 0,
        "rstd1": 2.25, "qkv": 0.75, "qk": 3, "v": 5.25, "cos": 2.25, "sin1": 4, "sin2": 3.5, "rope": 3.75,
        "exp": 4.75, "relu": 4.75, "phi": 5.25, "q_hi": 5.5, "k_hi": 6, "q_lo": 5.75, "k_lo": 6.25, "v1": 7.75,
        "vr": 6.75, "v2": 8.5, "v3": 8.75, "k_T": 6.25, "q_T": 5.75, "kT": 7.5, "qT0": 8.25, "qT1": 7.25,
        "qk0": 8.5, "qk1": 9.5, "qk2": 10.25, "qk3": 11, "mask0": 9.25, "mask1": 9.5, "mask2": 11,
        "mask3": 11.75, "a_hi0": 10.75, "a_hi1": 10.75, "a_hi2": 12.25, "a_hi3": 12.5, "a_lo0": 12.5,
        "a_lo1": 12.5, "a_lo2": 13.25, "a_lo3": 13.5, "av0": 13.25, "av1": 14, "o0": 14, "o1": 14.5,
        "state": 14.5, "st0_0": 16.5, "st0_1": 15.5, "st1_0": 15.25, "st1_1": 15.25, "ss": 18.25, "s1": 19.25,
        "sr": 20.75, "s2": 20.5, "s3": 22, "den": 14.6, "rec": 14.85, "norm": 15.1, "o_T": 16.25, "o_hi": 17.5,
        "o_lo": 16.75, "proj": -4, "x1": -2.25, "store_x1": 19.75, "mean2": -1, "xc": -0.75, "sq": 2.75,
        "var2": 1, "logit": 4.25, "v2n": 3.5, "r2n": 4.75, "rstd2": 3.25, "ln2": 6.25, "router": 6,
        "w_T": 13.25, "wt": 13.5, "store_w": 14, "x2_hi": -1.6, "x2_lo": -1.6,
    },
    "moe": {
        "load_x1": 28, "load_w": 15.75, "gate": -0.25, "up": 0, "tanh": 1.25, "g": 1.25, "h": 1.75, "gw": 3,
        "h_hi": 5, "h_lo": 6.5, "down": 6.5, "y": 5.75, "store_y": 9,
    },
}


class Part:

    def __init__(self, name):
        self.name = name
        self.ops = {e: [] for e in ENGINES}
        self.number = {}
        self.count = {}

    def add(self, engine, slot, event, fn, *waits):
        slot += PLACE[self.name][event if isinstance(event, str) else event[0]]
        late = int(slot // SLOTS)
        self.ops[engine].append((slot, late, event, fn, waits))

    def close(self):
        for engine, ops in self.ops.items():
            ops.sort(key=lambda op: op[0])
            for _, late, event, _, _ in ops:
                if isinstance(event, tuple):
                    n = self.count.get((late, engine), 0) + 1
                    self.count[late, engine] = n
                    self.number[engine, event] = late, n


ENGINES = ("tensor", "scalar", "vector", "gpsimd", "sync")


def bcast(ap, axis, n):
    ap = ap.unsqueeze(axis)
    shape = list(ap.shape)
    shape[axis] = n
    return ap.broadcast_to(shape)


def build(nc, x, xT, w_qkv, w_out, Wg, Wu, Wd, Wr, temperature, tab, outT, w_scr, x1_scr):
    ctx = ExitStack()

    def sb(name, shape, dt=F32):
        return ctx.enter_context(nc.sbuf_tensor(name, shape, dt))

    def sem(name):
        return ctx.enter_context(nc.semaphore(name))

    with ctx:
        ident = sb("ident", [P, P])
        ident16 = sb("ident16", [P, P], F16)
        cmask = sb("cmask", [P, P])
        mean_w = sb("mean_w", [P, P])
        iota = sb("iota", [P, E])
        iota_i = sb("iota_i", [P, E], mybir.dt.int32)
        temp = sb("temp", [P, 1])
        rtemp = sb("rtemp", [P, 1])
        mhalf = sb("mhalf", [P, NT])
        wqkv_p = [sb(f"wqkv_{s}", [P, KD, 3 * D], F32R) for s in ("hi", "lo")]
        wout_p = [sb(f"wout_{s}", [P, KD, D], F32R) for s in ("hi", "lo")]
        wg_p = [sb(f"wg_{s}", [P, E, KD, I], F32R) for s in ("hi", "lo")]
        wu_p = [sb(f"wu_{s}", [P, E, KD, I], F32R) for s in ("hi", "lo")]
        wd_p = [sb(f"wd_{s}", [P, E, KI, D], F32R) for s in ("hi", "lo")]
        wr_sb = sb("wr_sb", [P, KD, E])
        xraw = sb("xraw", [P, KD, B])
        xnat = sb("xnat", [P, 2, D])
        tabs = sb("tabs", [P, NT, 3 * HALF])
        xo = [sb(f"xo_{s}", [P, KD, B], F32R) for s in ("hi", "lo")]
        bst = sb("bst", [P, 6])
        idle = sb("idle", [P, 1])
        ve = sb("ve", [P, NT])
        v2n = sb("v2n", [P, NT])
        r2n = sb("r2n", [P, NT])
        mv = sb("mv", [P, NT, 2])
        rstd1 = sb("rstd1", [P, NT])
        qk = sb("qk", [P, 2 * D])
        rop = sb("rop", [P, 2 * D])
        rop2 = sb("rop2", [P, 2 * D])
        vs = sb("vs", [P, D])
        q_st = sb("q_st", [P, H, 4, HD], F16)
        k_st = sb("k_st", [P, 2, H, 4, HD], F16)
        kT = sb("kT", [P, NP, P], F16)
        qbd = sb("qbd", [P, NP, 2, P], F16)
        vx = sb("vx", [P, 2, H, 3, W1], BF16)
        am = sb("am", [P, 2, 4 * P])
        a_p = [sb(f"a_{s}", [P, H, P], F16) for s in ("hi", "lo")]
        osb = sb("osb", [P, H, W1])
        den = sb("den", [P, H])
        rec = sb("rec", [P, H])
        onrm = sb("onrm", [P, D])
        st_d = sb("st_d", [P, NP, W1])
        st_s = sb("st_s", [P, NP, W1])
        st_r = sb("st_r", [P, NP, W1])
        st_x = sb("st_x", [P, NP, 3, W1], BF16)
        x1 = sb("x1", [P, KD, B])
        sq = sb("sq", [P, B])
        rt = sq[0:E, :]
        R = {n: sb(f"r_{n}", [P, NT, E]) for n in
             ("z", "th", "inh", "zone", "zone2", "dist", "e1", "fb", "w0", "eq", "c", "s1", "nd", "s2", "fw", "w", "wo")}
        R1 = {n: sb(f"q_{n}", [P, NT]) for n in ("ws", "no", "yes", "m", "ix", "m2", "ix2", "w2")}
        x2 = [sb(f"x2_{s}", [P, KD, B], F32R) for s in ("hi", "lo")]
        x1r = sb("x1r", [P, KD, B])
        wb = sb("wb", [P, NWB, B])
        hb = sb("hb", [P, 2, B])
        h_p = [sb(f"h_{s}", [P, 2, B], F32R) for s in ("hi", "lo")]
        G, U, Y0, Y1, R0, R1b, R2, R3 = (
            ctx.enter_context(nc.psum_tensor(n, [P, 512], F32))
            for n in ("gate", "up", "y0", "y1", "front0", "front1", "back0", "back1"))
        Y, FR, BK = [Y0, Y1], [R0, R1b], [R2, R3]

        dma_names = ("c_temp", "c_wr", "c_wqkv", "c_wout", "x_raw", "x_nat0", "x_nat1", "tab", "x1_out", "w_out",
                     "x1_in", "y_out") + tuple(
                         f"{ring}{i}" for ring, n in (("wb", NWB), ("slab0", NWB), ("slab1", KD)) for i in range(n))
        carrier = sem("carrier")
        dsem = {n: sem(f"dma_{n}") for n in dma_names}

        setup, att, moe = (Part(n) for n in ("setup", "att", "moe"))
        parts = {"setup": setup, "att": att, "moe": moe}

        def at(part, engine, *event):
            return (part, engine, event, 0)

        def before(part, engine, *event):
            return (part, engine, event, 1)

        def dma(name, per_block, k, back=0):
            return ("dma", name, (per_block, k), back)

        def S(engine, *event):
            return at("setup", engine, *event)

        add = setup.add
        wq_raw = wb[:, :, :].rearrange("p a b -> p (a b)").rearrange("p (k n) -> p k n", k=KD)
        wo_raw = x1r[:, 0, :].rearrange("p (k n) -> p k n", k=KD)
        add("sync", 0, "load_w_qkv", lambda e, b: e.dma_start(wq_raw, w_qkv.rearrange("(k p) n -> p k n", p=P))
            .then_inc(dsem["c_wqkv"], 16))
        add("sync", 0, "load_w_out", lambda e, b: e.dma_start(wo_raw, w_out.rearrange("(k p) n -> p k n", p=P))
            .then_inc(dsem["c_wout"], 16))
        add("sync", 0, "load_Wr", lambda e, b: e.dma_start(wr_sb[:, :, :], Wr.rearrange("(k p) n -> p k n", p=P))
            .then_inc(dsem["c_wr"], 16))
        add("sync", 0, "load_temperature", lambda e, b: e.dma_start(temp[:, :], temperature.rearrange("(a n) -> a n", a=1)
                                                      .broadcast_to([P, 1])).then_inc(dsem["c_temp"], 16))
        add("vector", 0, ("ones",), lambda e, b: e.memset(mean_w[:, :], 1.0 / D))
        add("vector", 0, ("mhalf",), lambda e, b: e.memset(mhalf[:, :], -0.5))
        add("vector", 0, ("rtemp",), lambda e, b: e.reciprocal(rtemp[:, :], temp[:, :]), ("once", "c_temp", 1, 0))
        add("vector", 0, ("rtemp2",), lambda e, b: e.tensor_scalar(rtemp[:, :], rtemp[:, :], 0.5, None, ALU.mult),
            S("vector", "rtemp"))
        add("gpsimd", 0, ("id0",), lambda e, b: e.memset(ident[:, :], 0.0))
        add("gpsimd", 0, ("mask0",), lambda e, b: e.memset(cmask[:, :], ASCALE))
        add("gpsimd", 0, ("id",), lambda e, b: e.affine_select(
            out=ident[:, :], in_=ident[:, :], compare_op=ALU.not_equal, fill=1.0, base=0,
            pattern=[[-1, P]], channel_multiplier=1), S("gpsimd", "id0"))
        add("gpsimd", 0, ("mask",), lambda e, b: e.affine_select(
            out=cmask[:, :], in_=cmask[:, :], compare_op=ALU.is_ge, fill=0.0, base=0,
            pattern=[[1, P]], channel_multiplier=-1), S("gpsimd", "mask0"))
        add("gpsimd", 0, ("iota_i",), lambda e, b: e.iota(iota_i[:, :], pattern=[[1, E]], base=0, channel_multiplier=0))
        add("vector", 0, ("iota",), lambda e, b: e.tensor_copy(iota[:, :], iota_i[:, :]), S("gpsimd", "iota_i"))
        add("vector", 0, ("id16",), lambda e, b: e.tensor_copy(ident16[:, :], ident[:, :]), S("gpsimd", "id"))
        add("vector", 0, ("z_qbd",), lambda e, b: e.memset(qbd[:, :, :, :].rearrange("p a b c -> p (a b c)"), 0.0))
        add("vector", 0, ("z_vx",), lambda e, b: e.memset(vx[:, :, :, :, :].rearrange("p t a b c -> p (t a b c)"), 0.0))
        add("vector", 0, ("one_vx",), lambda e, b: e.memset(vx[:, :, :, 0, HD], 1.0), S("vector", "z_vx"))
        add("vector", 0, ("z_sx",), lambda e, b: e.memset(st_x[:, :, :, :].rearrange("p a b c -> p (a b c)"), 0.0))
        add("vector", 0, ("z_ss",), lambda e, b: e.memset(st_s[:, :, :].rearrange("p a b -> p (a b)"), 0.0))

        def col_means(e, b):
            for k in range(KD):
                e.matmul(R0[:, :], mean_w[:, :], wq_raw[:, k, 0:2 * D], start=(k == 0), stop=(k == KD - 1))
            for k in range(KD):
                m = e.matmul(R1b[:, 0:D], mean_w[:, :], wq_raw[:, k, 2 * D:], start=(k == 0), stop=(k == KD - 1))
            return m
        add("tensor", 0, ("colmean",), col_means, S("vector", "ones"), ("once", "c_wqkv", 1, 0))
        for k in range(KD):
            add("vector", 0, ("wc", k, 0), lambda e, b, k=k: e.tensor_tensor(
                wq_raw[:, k, 0:2 * D], wq_raw[:, k, 0:2 * D], R0[:, :], ALU.subtract), S("tensor", "colmean"))
            add("vector", 0, ("wc", k, 1), lambda e, b, k=k: e.tensor_tensor(
                wq_raw[:, k, 2 * D:], wq_raw[:, k, 2 * D:], R1b[:, 0:D], ALU.subtract), S("tensor", "colmean"))
            add("scalar", 0, ("wqkv_hi", k), lambda e, b, k=k: e.activation(
                wqkv_p[0][:, k, :], wq_raw[:, k, :], ACT.Copy), S("vector", "wc", k, 0), S("vector", "wc", k, 1))
            add("vector", 0, ("wqkv_lo", k), lambda e, b, k=k: e.tensor_tensor(
                wqkv_p[1][:, k, :], wq_raw[:, k, :], wqkv_p[0][:, k, :].bitcast(F32), ALU.subtract),
                S("scalar", "wqkv_hi", k))
        add("scalar", 0, ("wout_hi",), lambda e, b: e.activation(wout_p[0][:, :, :], wo_raw, ACT.Copy),
            ("once", "c_wout", 1, 0))
        add("vector", 0, ("wout_lo",), lambda e, b: e.tensor_tensor(
            wout_p[1][:, :, :], wo_raw, wout_p[0][:, :, :].bitcast(F32), ALU.subtract), S("scalar", "wout_hi"))

        slabs = [(src, dst, ex_) for ex_ in range(E) for src, dst in ((Wg, wg_p), (Wu, wu_p), (Wd, wd_p))]
        stages_of = [[wb[:, i, :] for i in range(NWB)], [x1r[:, i, :] for i in range(KD)]]

        def slab_done(n):
            return S("gpsimd" if n % 2 else "vector", "slab_lo", n)
        for n, (src, dst, ex_) in enumerate(slabs):
            late_one = n >= SLABS_WB
            ring = stages_of[late_one]
            i = n - SLABS_WB * late_one
            s, slot = i % len(ring), SLAB_STEP * n
            if i >= len(ring):
                free = [slab_done(n - len(ring))]
            elif late_one:
                free = [S("vector", "wout_lo")]
            else:
                free = [S("vector", "wqkv_lo", k) for k in range(KD)]
            dma_sem = f"slab{late_one:d}{s}"
            raw = ring[s].rearrange("p (k n) -> p k n", k=KD)
            add("sync", slot, "load_slab", lambda e, b, raw=raw, src=src, ex_=ex_, q=dma_sem: e.dma_start(
                raw, src[ex_].rearrange("(k p) n -> p k n", p=P)).then_inc(dsem[q], 16), *free)
            add("scalar", slot, ("slab_hi", n), lambda e, b, raw=raw, dst=dst, ex_=ex_: e.activation(
                dst[0][:, ex_, :, :], raw, ACT.Copy), ("once", dma_sem, i // len(ring) + 1, 0))
            add("gpsimd" if n % 2 else "vector", slot, ("slab_lo", n), lambda e, b, raw=raw, dst=dst, ex_=ex_: e.tensor_tensor(
                dst[1][:, ex_, :, :], raw, dst[0][:, ex_, :, :].bitcast(F32), ALU.subtract),
                S("scalar", "slab_hi", n))

        def A(engine, *event):
            return at("att", engine, *event)

        def Ab(engine, *event):
            return before("att", engine, *event)

        def An(engine, *event):
            return ("att", engine, event, -1)

        def M(engine, *event):
            return at("moe", engine, *event)

        def Mb(engine, *event):
            return before("moe", engine, *event)

        add = att.add

        add("sync", 0, "load_x", lambda e, b: e.dma_start(
            xraw[:, :, :], xT[:, bass.ds(b, B)].rearrange("(k p) n -> p k n", p=P)).then_inc(dsem["x_raw"], 16),
            Ab("vector", "x1", KD - 1))
        add("sync", 0, "load_tab", lambda e, b: e.dma_start(
            tabs[:, :, :], tab[bass.ds(b, B), :].rearrange("(t p) n -> p t n", p=P)).then_inc(dsem["tab"], 16),
            Ab("vector", "cos", NT - 1), Ab("gpsimd", "sin1", NT - 1), Ab("gpsimd", "sin2", NT - 1))

        for k in range(KD):
            add("scalar", 0, ("x_hi", k), lambda e, b, k=k: e.activation(xo[0][:, k, :], xraw[:, k, :], ACT.Copy),
                dma("x_raw", 1, 1), Ab("tensor", "proj"))
            add("vector", 0, ("x_lo", k), lambda e, b, k=k: e.tensor_tensor(
                xo[1][:, k, :], xraw[:, k, :], xo[0][:, k, :].bitcast(F32), ALU.subtract), A("scalar", "x_hi", k))

        for t in range(NT):
            f = TILE[t]
            tok = slice(t * P, (t + 1) * P)
            s = t % 2
            add("sync", f, "load_xnat", lambda e, b, t=t, s=s: e.dma_start(
                xnat[:, s, :], x[bass.ds(b + t * P, P), :]).then_inc(dsem[f"x_nat{s}"], 16),
                (A if t >= 2 else Ab)("vector", "bn", t - 2 if t >= 2 else t + 2))
            add("vector", f, ("bn", t), lambda e, b, s=s: e.bn_stats(bst[:, :], xnat[:, s, :]),
                dma(f"x_nat{s}", 2, t // 2 + 1), (A if t else Ab)("vector", "mv", t - 1 if t else NT - 1))
            add("vector", f, ("mv", t), lambda e, b, t=t: (e.memset(idle[:, :], 0.0), e.bn_aggr(mv[:, t, :], bst[:, :]))[-1],
                A("vector", "bn", t), Ab("gpsimd", "rstd1", t))
            add("vector", f, ("ve", t), lambda e, b, t=t: e.tensor_scalar(
                ve[:, t:t + 1], mv[:, t, 1:2], EPS, None, ALU.add), A("vector", "mv", t))
            add("gpsimd", f, ("rstd1", t), lambda e, b, t=t: e.tensor_tensor(
                rstd1[:, t:t + 1], ve[:, t:t + 1], mhalf[:, 0:1], ALU.pow),
                A("vector", "ve", t), Ab("scalar", "qk", t), Ab("scalar", "v", t), S("vector", "mhalf"))

            def qkv(e, b, tok=tok):
                n = 0
                for k in range(KD):
                    for xi, wis in ((0, (0, 1)), (1, (0,))):
                        for wi in wis:
                            lhs = xo[xi][:, k, tok]
                            first, last = n == 0, n == 3 * KD - 1
                            e.matmul(R0[:, :], lhs, wqkv_p[wi][:, k, 0:2 * D], start=first, stop=last)
                            m = e.matmul(R1b[:, 0:D], lhs, wqkv_p[wi][:, k, 2 * D:], start=first, stop=last)
                            n += 1
                return m
            prev_t = (lambda eng, *ev: A(eng, *ev, t - 1)) if t else (lambda eng, *ev: Ab(eng, *ev, NT - 1))
            prev2_t = (lambda eng, *ev: A(eng, *ev, t - 2)) if t >= 2 else (lambda eng, *ev: Ab(eng, *ev, NT + t - 2))
            add("tensor", f, ("qkv", t), qkv, A("scalar", "x_hi", KD - 1), A("vector", "x_lo", KD - 1),
                prev_t("vector", "kT"), prev_t("vector", "qT1"), prev_t("scalar", "qT0"),
                S("vector", "wqkv_lo", KD - 1))

            add("scalar", f, ("qk", t), lambda e, b, t=t: e.activation(
                qk[:, :], R0[:, :], ACT.Copy, scale=rstd1[:, t:t + 1]),
                A("tensor", "qkv", t), A("gpsimd", "rstd1", t), prev_t("vector", "q_lo"), prev_t("gpsimd", "k_lo"))
            add("scalar", f, ("v", t), lambda e, b, t=t: e.activation(
                vs[:, :], R1b[:, 0:D], ACT.Copy, scale=rstd1[:, t:t + 1]),
                A("tensor", "qkv", t), A("gpsimd", "rstd1", t), prev_t("gpsimd", "v3"))

            qk_h = qk[:, :].rearrange("p (h s d) -> p h s d", s=2, d=HALF)
            r2_h = rop2[:, :].rearrange("p (h s d) -> p h s d", s=2, d=HALF)
            add("vector", f, ("cos", t), lambda e, b, t=t: e.tensor_tensor(
                rop[:, :].rearrange("p (h d) -> p h d", d=HALF), qk[:, :].rearrange("p (h d) -> p h d", d=HALF),
                bcast(tabs[:, t, 0:HALF], 1, 4 * H), ALU.mult),
                A("scalar", "qk", t), dma("tab", 1, 1), prev_t("vector", "phi"))
            for s2, at_ in ((0, HALF), (1, 2 * HALF)):
                add("gpsimd", f, ("sin" + str(s2 + 1), t), lambda e, b, t=t, s2=s2, at_=at_: e.tensor_tensor(
                    r2_h[:, :, s2, :], qk_h[:, :, 1 - s2, :], bcast(tabs[:, t, at_:at_ + HALF], 1, 2 * H), ALU.mult),
                    A("scalar", "qk", t), dma("tab", 1, 1), prev_t("vector", "phi"))
            add("vector", f, ("rope", t), lambda e, b: e.tensor_tensor(rop[:, :], rop[:, :], rop2[:, :], ALU.add),
                A("vector", "cos", t), A("gpsimd", "sin1", t), A("gpsimd", "sin2", t))
            add("scalar", f, ("exp", t), lambda e, b: e.activation(rop2[:, :], rop[:, :], ACT.Exp),
                A("vector", "rope", t))
            add("scalar", f, ("relu", t), lambda e, b: e.activation(rop[:, :], rop[:, :], ACT.Relu),
                A("scalar", "exp", t))
            add("vector", f, ("phi", t), lambda e, b: e.scalar_tensor_tensor(
                out=qk[:, :], in0=rop2[:, :], scalar=1.0, in1=rop[:, :], op0=ALU.min, op1=ALU.add),
                A("scalar", "exp", t), A("scalar", "relu", t), A("gpsimd", "sin2", t), A("vector", "cos", t))
            f_q = bcast(qk[:, 0:D].rearrange("p (h d) -> p h d", d=HD), 2, 2)
            q_s, k_s, v_s = q_st[:, :, :, :], k_st[:, t % 2, :, :, :], vx[:, t % 2, :, :, :]
            f_k = bcast(qk[:, D:].rearrange("p (h d) -> p h d", d=HD), 2, 2)
            add("scalar", f, ("q_hi", t), lambda e, b, f_q=f_q: e.activation(q_s[:, :, 0:2, :], f_q, ACT.Copy),
                A("vector", "phi", t), prev_t("tensor", "q_T"))
            add("scalar", f, ("k_hi", t), lambda e, b, f_k=f_k, k_s=k_s: e.activation(k_s[:, :, 0::2, :], f_k, ACT.Copy),
                A("vector", "phi", t), prev2_t("tensor", "state"))
            add("vector", f, ("q_lo", t), lambda e, b, f_q=f_q: e.tensor_tensor(
                q_s[:, :, 2:4, :], f_q, q_s[:, :, 0:2, :], ALU.subtract), A("scalar", "q_hi", t))
            add("gpsimd", f, ("k_lo", t), lambda e, b, f_k=f_k, k_s=k_s: e.tensor_tensor(
                k_s[:, :, 1::2, :], f_k, k_s[:, :, 0::2, :], ALU.subtract), A("scalar", "k_hi", t))
            v_h = vs[:, :].rearrange("p (h d) -> p h d", d=HD)
            add("scalar", f, ("v1", t), lambda e, b, v_s=v_s: e.activation(v_s[:, :, 0, 0:HD], v_h, ACT.Copy),
                A("scalar", "v", t), prev2_t("tensor", "state"), S("vector", "z_vx"))
            add("gpsimd", f, ("vr", t), lambda e, b, v_s=v_s: e.tensor_tensor(v_h, v_h, v_s[:, :, 0, 0:HD], ALU.subtract),
                A("scalar", "v1", t))
            add("scalar", f, ("v2", t), lambda e, b, v_s=v_s: e.activation(v_s[:, :, 1, 0:HD], v_h, ACT.Copy),
                A("gpsimd", "vr", t))
            add("gpsimd", f, ("v3", t), lambda e, b, v_s=v_s: e.tensor_tensor(
                v_s[:, :, 2, 0:HD], v_h, v_s[:, :, 1, 0:HD], ALU.subtract), A("scalar", "v2", t))

            kTp, qTp = (r[:, :].bitcast(F16).rearrange("p (a b) -> p a b", a=NP) for r in (R0, R1b))

            def turn(e, dst, heads):
                for p in range(NP):
                    m = e.transpose(dst[:, p, :], heads[:, 2 * p:2 * p + 2, :, :]
                                    .rearrange("p h c d -> p (h c d)"), ident16[:, :])
                return m
            add("tensor", f, ("k_T", t), lambda e, b, d=kTp, k_s=k_s: turn(e, d, k_s),
                A("scalar", "k_hi", t), A("gpsimd", "k_lo", t), A("scalar", "qk", t), S("vector", "id16"),
                *((Ab("scalar", "wt"),) if t == 1 else ()))
            add("tensor", f, ("q_T", t), lambda e, b, d=qTp: turn(e, d, q_s),
                A("scalar", "q_hi", t), A("vector", "q_lo", t), A("scalar", "v", t), S("vector", "id16"))
            add("vector", f, ("kT", t), lambda e, b, s_=kTp: e.tensor_copy(kT[:, :, :], s_),
                A("tensor", "k_T", t), *[prev_t("tensor", f"qk{r}") for r in range(4)])
            add("scalar", f, ("qT0", t), lambda e, b, s_=qTp: e.activation(qbd[0:64, :, 0, :], s_[0:64], ACT.Copy),
                A("tensor", "q_T", t), prev_t("tensor", "av0"), prev_t("tensor", "av1"), S("vector", "z_qbd"))
            add("vector", f, ("qT1", t), lambda e, b, s_=qTp: e.tensor_copy(qbd[64:P, :, 1, :], s_[64:P]),
                A("tensor", "q_T", t), prev_t("tensor", "av0"), prev_t("tensor", "av1"), S("vector", "z_qbd"))

            for r in range(4):
                bank = BK[r % 2]
                if r >= 2:
                    free = (A("vector", f"mask{r - 2}", t),)
                elif t:
                    free = tuple(A("vector", f"st{r}_{hh}", t - 1) for hh in range(2)) + (
                        (A("vector", "o_lo", t - 1),) if r else ())
                else:
                    free = (Ab("vector", "ln2", KD - 1),) if r else (Ab("vector", "router", "z"),)
                add("tensor", f, (f"qk{r}", t), lambda e, b, r=r, bank=bank: [e.matmul(
                    bank[:, 2 * P * j:2 * P * (j + 1)], kT[:, 2 * r + j, :],
                    qbd[:, 2 * r + j, :, :].rearrange("p a b -> p (a b)"), start=True, stop=True)
                    for j in range(2)][-1],
                    A("vector", "kT", t), A("vector", "qT1", t), A("scalar", "qT0", t), *free)
                add("vector", f, (f"mask{r}", t), lambda e, b, r=r, bank=bank: e.tensor_tensor(
                    am[:, r % 2, :].rearrange("p (h n) -> p h n", h=4), bank[:, :].rearrange("p (h n) -> p h n", h=4),
                    bcast(cmask[:, :], 1, 4), ALU.mult),
                    A("tensor", f"qk{r}", t), S("gpsimd", "mask"),
                    A("gpsimd", f"a_lo{r - 2}", t) if r >= 2 else prev_t("gpsimd", f"a_lo{r + 2}"))
                a4 = am[:, r % 2, :].rearrange("p (h n) -> p h n", h=4)
                add("scalar", f, (f"a_hi{r}", t), lambda e, b, r=r, a4=a4: e.activation(
                    a_p[0][:, 4 * r:4 * r + 4, :], a4, ACT.Copy),
                    A("vector", f"mask{r}", t), prev_t("tensor", f"av{r // 2}"))
                add("gpsimd", f, (f"a_lo{r}", t), lambda e, b, r=r, a4=a4: e.tensor_tensor(
                    a_p[1][:, 4 * r:4 * r + 4, :], a4, a_p[0][:, 4 * r:4 * r + 4, :], ALU.subtract),
                    A("scalar", f"a_hi{r}", t))

            def attend(e, g, v_s):
                for h in range(8 * g, 8 * g + 8):
                    o = BK[g][:, (h % 8) * WV:(h % 8 + 1) * WV]
                    e.matmul(o, qbd[:, h // 2, h % 2, :], st_x[:, h // 2, :, :].rearrange("p a b -> p (a b)"),
                             start=(h % 8 == 0), stop=False, skip_group_check=True)
                for h in range(8 * g, 8 * g + 8):
                    o = BK[g][:, (h % 8) * WV:(h % 8 + 1) * WV]
                    for a in a_p:
                        m = e.matmul(o, a[:, h, :], v_s[:, h, :, :].rearrange("p a b -> p (a b)"),
                                     start=False, stop=(h % 8 == 7), skip_group_check=True)
                return m
            for g in range(2):
                add("tensor", f, (f"av{g}", t), lambda e, b, g=g, v_s=v_s: attend(e, g, v_s),
                    A("vector", f"mask{2 + g}", t), A("gpsimd", f"a_lo{2 * g}", t), A("scalar", f"a_hi{2 * g}", t),
                    A("gpsimd", f"a_lo{2 * g + 1}", t), A("scalar", f"a_hi{2 * g + 1}", t),
                    A("gpsimd", "v3", t), A("scalar", "v2", t),
                    prev_t("gpsimd", "s3"), prev_t("scalar", "s2"), S("vector", "z_sx"), S("vector", "one_vx"))
                add("vector", f, (f"o{g}", t), lambda e, b, g=g: e.tensor_reduce(
                    osb[:, 8 * g:8 * g + 8, :],
                    BK[g][:, 0:8 * WV].rearrange("p (h s d) -> p h d s", s=3, d=W1), AX.X, ALU.add),
                    A("tensor", f"av{g}", t), prev_t("vector", "norm"))

            def state(e, b, k_s=k_s, v_s=v_s):
                for p in range(NP):
                    m = e.matmul(BK[p // 4][:, (p % 4) * 2 * WV:(p % 4 + 1) * 2 * WV],
                                 k_s[:, 2 * p:2 * p + 2, :, :].rearrange("p h c d -> p (h c d)"),
                                 v_s[:, 2 * p:2 * p + 2, :, :].rearrange("p h a b -> p (h a b)"),
                                 start=(p % 4 == 0), stop=(p % 4 == 3), skip_group_check=True)
                return m
            add("tensor", f, ("state", t), state, A("vector", "o0", t), A("vector", "o1", t))
            for g in range(2):
                for hh in range(2):
                    rows = slice(64 * hh, 64 * hh + 64)
                    add("vector", f, (f"st{g}_{hh}", t),
                        lambda e, b, g=g, hh=hh, rows=rows: e.tensor_reduce(
                            st_d[rows, 4 * g:4 * g + 4, :],
                            BK[g][rows, 0:8 * WV].rearrange("p (q h s d) -> p q h d s", h=2, s=3, d=W1)[:, :, hh, :, :],
                            AX.X, ALU.add), A("tensor", "state", t), prev_t("vector", "ss"))
            add("vector", f, ("ss", t), lambda e, b: e.scalar_tensor_tensor(
                out=st_s[:, :, :], in0=st_d[:, :, :], scalar=ASCALE, in1=st_s[:, :, :], op0=ALU.mult, op1=ALU.add),
                A("vector", "st1_1", t), A("vector", "st0_0", t), A("vector", "st0_1", t), A("vector", "st1_0", t),
                prev_t("gpsimd", "sr"), prev_t("scalar", "s1"), S("vector", "z_ss"))
            add("scalar", f, ("s1", t), lambda e, b: e.activation(st_x[:, :, 0, :], st_s[:, :, :], ACT.Copy),
                A("vector", "ss", t), A("tensor", "av0", t), A("tensor", "av1", t), S("vector", "z_sx"))
            add("gpsimd", f, ("sr", t), lambda e, b: e.tensor_tensor(
                st_r[:, :, :], st_s[:, :, :], st_x[:, :, 0, :], ALU.subtract), A("scalar", "s1", t),
                prev_t("gpsimd", "s3"))
            add("scalar", f, ("s2", t), lambda e, b: e.activation(st_x[:, :, 1, :], st_r[:, :, :], ACT.Copy),
                A("gpsimd", "sr", t))
            add("gpsimd", f, ("s3", t), lambda e, b: e.tensor_tensor(
                st_x[:, :, 2, :], st_r[:, :, :], st_x[:, :, 1, :], ALU.subtract), A("scalar", "s2", t))

            add("vector", f, ("den", t), lambda e, b: e.tensor_scalar(
                den[:, :], osb[:, :, HD], 1.0 / ASCALE, 1e-6, ALU.mult, ALU.max),
                A("vector", "o0", t), A("vector", "o1", t), prev_t("vector", "rec"))
            add("vector", f, ("rec", t), lambda e, b: e.reciprocal(rec[:, :], den[:, :]), A("vector", "den", t))
            add("vector", f, ("norm", t), lambda e, b: e.scalar_tensor_tensor(
                out=onrm[:, :].rearrange("p (h d) -> p h d", d=HD), in0=osb[:, :, 0:HD], scalar=1.0 / ASCALE,
                in1=bcast(rec[:, :], 2, HD), op0=ALU.mult, op1=ALU.mult),
                A("vector", "rec", t), prev_t("tensor", "o_T"))
            add("tensor", f, ("o_T", t), lambda e, b: [e.transpose(
                R3[:, k * P:(k + 1) * P], onrm[:, k * P:(k + 1) * P], ident[:, :]) for k in range(KD)][-1],
                A("vector", "norm", t), A("vector", "st1_0", t), A("vector", "st1_1", t), S("gpsimd", "id"))
            oT = R3[:, 0:D].rearrange("p (k n) -> p k n", k=KD)
            add("scalar", f, ("o_hi", t), lambda e, b, tok=tok, oT=oT: e.activation(xo[0][:, :, tok], oT, ACT.Copy),
                A("tensor", "o_T", t))
            add("vector", f, ("o_lo", t), lambda e, b, tok=tok, oT=oT: e.tensor_tensor(
                xo[1][:, :, tok], oT, xo[0][:, :, tok].bitcast(F32), ALU.subtract), A("scalar", "o_hi", t))

        z = Z0

        def proj(e, b):
            for m_ in range(KD):
                n = 0
                for k in range(KD):
                    for wi, xi in ((0, 0), (1, 0), (0, 1)):
                        mm = e.matmul(BK[m_][:, :], wout_p[wi][:, k, m_ * P:(m_ + 1) * P], xo[xi][:, k, :],
                                      start=(n == 0), stop=(n == 3 * KD - 1))
                        n += 1
            return mm
        add("tensor", z, ("proj",), proj, A("scalar", "o_hi", NT - 1), A("vector", "o_lo", NT - 1),
            A("vector", "st0_0", NT - 1), A("vector", "st0_1", NT - 1),
            S("vector", "wout_lo"))
        for k in range(KD):
            add("vector", z, ("x1", k), lambda e, b, k=k: e.tensor_tensor(x1[:, k, :], BK[k][:, :], xraw[:, k, :], ALU.add),
                A("tensor", "proj"), Ab("scalar", "x2_hi", k), Ab("vector", "x2_lo", k))
        add("sync", z, "store_x1", lambda e, b: e.dma_start(x1_scr.rearrange("(k p) n -> p k n", p=P), x1[:, :, :])
            .then_inc(dsem["x1_out"], 16), A("vector", "x1", KD - 1), dma("x1_in", 1, 1, 1))
        add("tensor", z, ("mean2",), lambda e, b: [e.matmul(
            R2[:, :], mean_w[:, :], x1[:, k, :], start=(k == 0), stop=(k == KD - 1)) for k in range(KD)][-1],
            A("vector", "x1", 0), A("vector", "x1", 1))
        for k in range(KD):
            add("vector", z, ("xc", k), lambda e, b, k=k: e.tensor_tensor(
                x1[:, k, :], x1[:, k, :], R2[:, :], ALU.subtract), A("tensor", "mean2"), dma("x1_out", 1, 1))
            add("scalar", z, ("sq", k), lambda e, b, k=k: e.activation(sq[:, :], x1[:, k, :], ACT.Square),
                A("vector", "xc", k), A("tensor", "var2", k - 1) if k else dma("w_out", 1, 1, 1))
            add("tensor", z + k, ("var2", k), lambda e, b, k=k: [e.matmul(
                R3[:, t:t + 1], sq[:, t * P:(t + 1) * P], mean_w[:, 0:1], start=(k == 0 and t == 0),
                stop=(k == KD - 1 and t == NT - 1), skip_group_check=True) for t in range(NT)][-1],
                A("scalar", "sq", k), A("vector", "x1", 1))
        add("tensor", z, ("logit",), lambda e, b: [e.matmul(
            R2[:, t * E:(t + 1) * E], x1[:, k, t * P:(t + 1) * P], wr_sb[:, k, :], start=(k == 0 and t == 0),
            stop=(k == KD - 1 and t == NT - 1), skip_group_check=True) for k in range(KD) for t in range(NT)][-1],
            A("vector", "xc", 0), A("vector", "xc", 1), ("once", "c_wr", 1, 0))
        add("vector", z, ("v2n",), lambda e, b: e.tensor_scalar(v2n[:, :], R3[:, 0:NT], EPS, None, ALU.add),
            A("tensor", "var2", KD - 1))
        add("gpsimd", z, ("r2n",), lambda e, b: e.tensor_tensor(r2n[:, :], v2n[:, :], mhalf[:, :], ALU.pow),
            A("vector", "v2n"))
        add("tensor", z, ("rstd2",), lambda e, b: [e.transpose(
            R3[:, t * P:(t + 1) * P], r2n[:, t:t + 1].broadcast_to([P, P]), ident[:, :]) for t in range(NT)][-1],
            A("gpsimd", "r2n"))
        for k in range(KD):
            add("vector", z, ("ln2", k), lambda e, b, k=k: e.tensor_tensor(
                x1[:, k, :], x1[:, k, :], R3[:, :], ALU.mult), A("tensor", "rstd2"), A("tensor", "logit"))

        r_ = {n: v[:, :, :] for n, v in R.items()}
        q_ = {n: v[:, :] for n, v in R1.items()}
        lg = R2[:, 0:NT * E].rearrange("p (t n) -> p t n", n=E)
        io = bcast(iota[:, :], 1, NT)
        V = "vector"
        steps = [
            (V, "z", lambda e: e.tensor_tensor(r_["z"], lg, bcast(r2n[:, :], 2, E), ALU.mult), ()),
            ("scalar", "th", lambda e: e.activation(r_["th"], r_["z"], ACT.Tanh, scale=rtemp[:, 0:1]), ("z",)),
            (V, "inh", lambda e: e.tensor_scalar(r_["inh"], r_["th"], 0.5, 0.5, ALU.mult, ALU.add), ("th",)),
            (V, "off", lambda e: e.tensor_scalar(r_["nd"], r_["inh"], G_CENTER, None, ALU.subtract), ("inh",)),
            (V, "zone", lambda e: e.tensor_scalar(r_["zone"], r_["inh"], G_LOWER, None, ALU.is_ge), ("inh",)),
            (V, "dist", lambda e: e.scalar_tensor_tensor(
                out=r_["dist"], in0=r_["nd"], scalar=-1.0, in1=r_["nd"], op0=ALU.mult, op1=ALU.max), ("off",)),
            ("scalar", "e1", lambda e: e.activation(r_["e1"], r_["dist"], ACT.Exp, scale=-1.0 / 0.1), ("dist",)),
            ("scalar", "fb", lambda e: e.activation(r_["fb"], r_["dist"], ACT.Exp, scale=-1.0 / 0.3), ("dist",)),
            (V, "zone2", lambda e: e.scalar_tensor_tensor(
                out=r_["zone2"], in0=r_["inh"], scalar=G_UPPER, in1=r_["zone"], op0=ALU.is_le, op1=ALU.mult), ("zone",)),
            (V, "m", lambda e: e.tensor_reduce(q_["m"], r_["dist"], AX.X, ALU.min), ("dist",)),
            (V, "eq", lambda e: e.tensor_tensor(r_["eq"], r_["dist"], bcast(q_["m"], 2, E), ALU.not_equal), ("m",)),
            (V, "w0", lambda e: e.tensor_tensor(r_["w0"], r_["e1"], r_["zone2"], ALU.mult), ("e1", "zone2")),
            (V, "c", lambda e: e.scalar_tensor_tensor(
                out=r_["c"], in0=r_["eq"], scalar=99.0, in1=io, op0=ALU.mult, op1=ALU.add), ("eq",)),
            (V, "ws", lambda e: e.tensor_reduce(q_["ws"], r_["w0"], AX.X, ALU.add), ("w0",)),
            (V, "ix", lambda e: e.tensor_reduce(q_["ix"], r_["c"], AX.X, ALU.min), ("c",)),
            (V, "no", lambda e: e.tensor_scalar(q_["no"], q_["ws"], 1e-8, None, ALU.is_lt), ("ws",)),
            (V, "s1", lambda e: e.tensor_tensor(r_["s1"], io, bcast(q_["ix"], 2, E), ALU.is_equal), ("ix",)),
            (V, "yes", lambda e: e.tensor_scalar(q_["yes"], q_["ws"], 1e-8, None, ALU.is_ge), ("ws",)),
            (V, "nd", lambda e: e.scalar_tensor_tensor(
                out=r_["nd"], in0=r_["s1"], scalar=9.0, in1=r_["dist"], op0=ALU.mult, op1=ALU.add), ("s1",)),
            (V, "w1", lambda e: e.tensor_tensor(r_["w0"], r_["w0"], bcast(q_["yes"], 2, E), ALU.mult), ("yes",)),
            (V, "m2", lambda e: e.tensor_reduce(q_["m2"], r_["nd"], AX.X, ALU.min), ("nd",)),
            (V, "fbn", lambda e: e.tensor_tensor(r_["fw"], r_["fb"], bcast(q_["no"], 2, E), ALU.mult), ("fb", "no")),
            (V, "eq2", lambda e: e.tensor_tensor(r_["eq"], r_["nd"], bcast(q_["m2"], 2, E), ALU.not_equal), ("m2", "c")),
            (V, "c2", lambda e: e.scalar_tensor_tensor(
                out=r_["c"], in0=r_["eq"], scalar=99.0, in1=io, op0=ALU.mult, op1=ALU.add), ("eq2",)),
            (V, "ix2", lambda e: e.tensor_reduce(q_["ix2"], r_["c"], AX.X, ALU.min), ("c2",)),
            (V, "s2", lambda e: e.tensor_tensor(r_["s2"], io, bcast(q_["ix2"], 2, E), ALU.is_equal), ("ix2",)),
            (V, "s12", lambda e: e.tensor_tensor(r_["s1"], r_["s1"], r_["s2"], ALU.add), ("s2",)),
            (V, "fw", lambda e: e.tensor_tensor(r_["fw"], r_["fw"], r_["s1"], ALU.mult), ("s12", "fbn")),
            (V, "w", lambda e: e.tensor_tensor(r_["w"], r_["w0"], r_["fw"], ALU.add), ("fw", "w1")),
            (V, "w2", lambda e: e.tensor_reduce(q_["w2"], r_["w"], AX.X, ALU.add), ("w",)),
            (V, "w3", lambda e: e.tensor_scalar(q_["w2"], q_["w2"], 1e-8, 2.0, ALU.max, ALU.mult), ("w2",)),
            (V, "w4", lambda e: e.reciprocal(q_["w2"], q_["w2"]), ("w3",)),
            (V, "wo", lambda e: e.tensor_tensor(r_["wo"], r_["w"], bcast(q_["w2"], 2, E), ALU.mult), ("w4",)),
        ]
        made_by = {name: eng for eng, name, _, _ in steps}
        for n, (eng, name, fn, needs) in enumerate(steps):
            waits = [A(made_by[need], "router", need) for need in needs]
            if name == "z":
                waits += [A("tensor", "logit"), A("gpsimd", "r2n")]
            if name == "th":
                waits += [S("vector", "rtemp2")]
            if name == "inh":
                waits += [Ab("tensor", "w_T"), S("vector", "iota")]
            add(eng, z + n * 0.13, ("router", name), lambda e, b, fn=fn: fn(e), *waits)
        add("tensor", z, ("w_T",), lambda e, b: [e.transpose(
            R0[0:E, t * P:(t + 1) * P], R["wo"][:, t, :], ident[:, :]) for t in range(NT)][-1],
            A("vector", "router", "wo"), An("scalar", "qk", 1))
        add("scalar", z, ("wt",), lambda e, b: e.activation(rt, R0[0:E, :], ACT.Copy), A("tensor", "w_T"),
            dma("w_out", 1, 1, 1))
        add("scalar", z, "store_w", lambda e, b: e.dma_start(w_scr, rt).then_inc(dsem["w_out"], 16),
            A("scalar", "wt"), *[dma(f"wb{i}", len(range(i, E, NWB)), len(range(i, E, NWB)), 1) for i in range(NWB)])

        for k in range(KD):
            att.add("scalar", M0, ("x2_hi", k), lambda e, b, k=k: e.activation(x2[0][:, k, :], x1[:, k, :], ACT.Copy),
                A("vector", "ln2", k), Mb("tensor", "gate", UNITS - 1), Mb("tensor", "up", UNITS - 1))
            att.add("vector", M0, ("x2_lo", k), lambda e, b, k=k: e.tensor_tensor(
                x2[1][:, k, :], x1[:, k, :], x2[0][:, k, :].bitcast(F32), ALU.subtract), A("scalar", "x2_hi", k))

        add = moe.add
        add("sync", M0, "load_x1", lambda e, b: e.dma_start(x1r[:, :, :], x1_scr.rearrange("(k p) n -> p k n", p=P))
            .then_inc(dsem["x1_in"], 16), dma("x1_out", 1, 1), dma("y_out", 1, 1, 1),
            *[slab_done(len(slabs) - 1 - i) for i in range(KD)])
        for e_ in range(E):
            s, n = e_ % NWB, e_ // NWB + 1
            cnt = len(range(s, E, NWB))
            if e_ < NWB:
                last_use = max(x_ for x_ in range(E) if x_ % NWB == s)
                free = [Mb("vector", "gw", 2 * last_use + 1)] + [slab_done(SLABS_WB - 1 - i) for i in range(NWB)]
            else:
                free = [M("vector", "gw", 2 * (e_ - NWB) + 1)]
            add("sync", M0 + max(0, 6 * (e_ - NWB) + 8), "load_w", lambda e, b, e_=e_, s=s: e.dma_start(
                wb[:, s, :], w_scr[e_:e_ + 1, :].broadcast_to([P, B])).then_inc(dsem[f"wb{s}"], 16),
                dma("w_out", 1, 1), *free)

        def three(e, out, w, wsel, xs, xsel, start, stop):
            todo = [(wi, xi, k) for wi, xi in ((0, 0), (1, 0), (0, 1)) for k in range(len(wsel))]
            for n, (wi, xi, k) in enumerate(todo):
                m = e.matmul(out, wsel[k](w[wi]), xsel[k](xs[xi]), start=start and n == 0,
                             stop=stop and n == len(todo) - 1, skip_group_check=not (start and stop))
            return m

        for u in range(UNITS):
            e_, m_ = u // KI, u % KI
            c = slice(m_ * P, (m_ + 1) * P)
            hs = u % 2
            prv = (lambda eng, ev, d=1: M(eng, ev, u - d) if u >= d else Mb(eng, ev, UNITS + u - d))
            wsel = [lambda w, k=k, e_=e_, c=c: w[:, e_, k, c] for k in range(KD)]
            xsel = [lambda x_, k=k: x_[:, k, :] for k in range(KD)]
            add("tensor", M0 + 3 * u, ("gate", u), lambda e, b, wsel=wsel, xsel=xsel: three(
                e, G[:, :], wg_p, wsel, x2, xsel, True, True),
                prv("vector", "g"), A("scalar", "x2_hi", KD - 1), A("vector", "x2_lo", KD - 1), slab_done(3 * e_))
            add("tensor", M0 + 3 * u, ("up", u), lambda e, b, wsel=wsel, xsel=xsel: three(
                e, U[:, :], wu_p, wsel, x2, xsel, True, True), prv("vector", "h"),
                A("scalar", "x2_hi", KD - 1), A("vector", "x2_lo", KD - 1), slab_done(3 * e_ + 1))
            add("scalar", M0 + 3 * u, ("tanh", u), lambda e, b, hs=hs: e.activation(hb[:, hs, :], G[:, :], ACT.Tanh, scale=0.5),
                M("tensor", "gate", u), prv("gpsimd", "h_lo", 2), prv("scalar", "h_hi", 2))
            add("vector", M0 + 3 * u, ("g", u), lambda e, b, hs=hs: e.scalar_tensor_tensor(
                out=hb[:, hs, :], in0=hb[:, hs, :], scalar=1.0, in1=G[:, :], op0=ALU.add, op1=ALU.mult),
                M("scalar", "tanh", u))
            add("vector", M0 + 3 * u, ("h", u), lambda e, b, hs=hs: e.tensor_tensor(
                hb[:, hs, :], hb[:, hs, :], U[:, :], ALU.mult), M("vector", "g", u), M("tensor", "up", u))
            add("vector", M0 + 3 * u, ("gw", u), lambda e, b, hs=hs, e_=e_: e.tensor_tensor(
                hb[:, hs, :], hb[:, hs, :], wb[:, e_ % NWB, :], ALU.mult),
                M("vector", "h", u), dma(f"wb{e_ % NWB}", len(range(e_ % NWB, E, NWB)), e_ // NWB + 1))
            add("scalar", M0 + 3 * u, ("h_hi", u), lambda e, b, hs=hs: e.activation(h_p[0][:, hs, :], hb[:, hs, :], ACT.Copy),
                M("vector", "gw", u), prv("tensor", "down", 2))
            add("gpsimd", M0 + 3 * u, ("h_lo", u), lambda e, b, hs=hs: e.tensor_tensor(
                h_p[1][:, hs, :], hb[:, hs, :], h_p[0][:, hs, :].bitcast(F32), ALU.subtract),
                M("scalar", "h_hi", u), prv("tensor", "down", 2))

            def down(e, b, u=u, e_=e_, m_=m_, hs=hs):
                for wi, hi in ((0, 0), (1, 0), (0, 1)):
                    for d in range(KD):
                        mm = e.matmul(Y[d][:, :], wd_p[wi][:, e_, m_, d * P:(d + 1) * P], h_p[hi][:, hs, :],
                                      start=(u == 0 and (wi, hi) == (0, 0)),
                                      stop=(u == UNITS - 1 and hi == 1), skip_group_check=True)
                return mm
            waits = [M("scalar", "h_hi", u), M("gpsimd", "h_lo", u), slab_done(3 * e_ + 2)]
            if u == 0:
                waits += [Mb("vector", "y", k) for k in range(KD)]
            add("tensor", M0 + 3 * u, ("down", u), down, *waits)
        for k in range(KD):
            add("vector", M0 + SLOTS, ("y", k), lambda e, b, k=k: e.tensor_tensor(
                x1r[:, k, :], Y[k][:, :], x1r[:, k, :], ALU.add), M("tensor", "down", UNITS - 1), dma("x1_in", 1, 1))
        add("scalar", M0 + SLOTS, "store_y", lambda e, b: e.dma_start(
            outT[:, bass.ds(b, B)].rearrange("(k p) n -> p k n", p=P), x1r[:, :, :]).then_inc(dsem["y_out"], 16),
            M("vector", "y", KD - 1))

        for part in parts.values():
            part.close()
        LATE = max(late for part in parts.values() for late, _ in part.count)
        sems = {(part.name, late, e): sem(f"{part.name}{late}_{e}")
                for part in parts.values() for late, e in part.count}

        def emit(engine, eng, stage, first, last, constants):
            merged = []
            for n, (name, part) in enumerate(parts.items()):
                for slot, late, event, fn, waits in part.ops[engine]:
                    if (first == last == late) if name == "setup" else (0 <= first - late and last - late < NB):
                        merged.append((slot - late * SLOTS, n, name, late, event, fn, waits))
            merged.sort(key=lambda x_: x_[:2])
            seen = {key: known for key, known in constants.items()}
            rows = {late: (stage - late) * B if isinstance(stage, int) else eng.snap((stage - late) * B)
                    for late in range(LATE + 1)} if engine in ("sync", "scalar") else {}
            for _, _, name, late, event, fn, waits in merged:
                b = stage - late if name != "setup" else 0
                todo = []
                for kind, producer, w_event, back in waits:
                    if isinstance(b, int) and b - back >= NB:
                        continue
                    if kind == "once":
                        sm, per, rel = dsem[producer], 0, 16 * w_event
                    elif kind == "dma":
                        (n, k) = w_event
                        sm, per, rel = dsem[producer], 16 * n, 16 * (k + ((producer == "y_out") - back) * n)
                    else:
                        its, number = parts[kind].number[producer, w_event]
                        n = parts[kind].count[its, producer] if kind != "setup" else 0
                        sm, per = sems[kind, its, producer], n
                        rel = number + (1 - back) * n
                    value = b * per + rel
                    if isinstance(value, int):
                        if value <= 0:
                            continue
                        key, known = sm.name, value
                        if kind in ("setup", "once"):
                            constants[key] = max(value, constants.get(key, 0))
                    else:
                        key, known = (sm.name, late, per == 0), rel
                    if seen.get(key, 0) < known or key not in seen:
                        seen[key] = known
                        todo.append((sm, value))
                for n, (sm, value) in enumerate(todo):
                    eng.wait_ge(sm, value)
                    if engine == "sync" and not isinstance(b, int):
                        eng.sem_inc(carrier, 1)
                ins = fn(eng, rows.get(late) if isinstance(event, str) else b)
                if isinstance(event, tuple):
                    ins.then_inc(sems[name, late, engine], 1)

        def program(engine):
            def run(eng):
                for (name, late, owner), sm in sems.items():
                    if owner == engine and name != "setup":
                        eng.sem_inc(sm, parts[name].count[late, owner])
                if engine == "sync":
                    eng.sem_inc(dsem["y_out"], 16)
                constants = {}
                for stage in range(LATE):
                    emit(engine, eng, stage, stage, stage, constants)
                with eng.Fori(LATE, NB) as i:
                    emit(engine, eng, i, LATE, NB - 1, constants)
                for stage in range(NB, NB + LATE):
                    emit(engine, eng, stage, stage, stage, constants)
                if engine == "sync":
                    for n in ("x1_out", "w_out", "y_out"):
                        eng.wait_ge(dsem[n], 16 * (NB + (n == "y_out")))
            return run

        block = ctx.enter_context(nc.Block())
        block.tensor(program("tensor"))
        block.scalar(program("scalar"))
        block.vector(program("vector"))
        block.gpsimd(program("gpsimd"))
        block.sync(program("sync"))


def kernel(**inputs):
    import concourse.bacc as bacc
    from concourse.bass_utils import run_bass_kernel_spmd

    x = np.asarray(inputs["L0_attn_x"])
    inv_freq = (np.float32(1.0) / np.power(np.float32(10000.0), np.arange(HALF, dtype=np.float32) / np.float32(HALF)))
    ang = (np.arange(N, dtype=np.float32)[:, None] * inv_freq.astype(np.float32)[None, :]).astype(np.float64)
    cos, sin = (f(ang).astype(np.float32) * np.float32(SCALE) for f in (np.cos, np.sin))
    arrays = {
        "x": np.ascontiguousarray(x[0]),
        "xT": np.ascontiguousarray(x[0].T),
        "w_qkv": np.ascontiguousarray(inputs["L0_attn_w_qkv"]),
        "w_out": np.ascontiguousarray(inputs["L0_attn_w_out"]),
        "Wg": np.ascontiguousarray(inputs["L0_ffn_Wg"]),
        "Wu": np.ascontiguousarray(inputs["L0_ffn_Wu"]),
        "Wd": np.ascontiguousarray(inputs["L0_ffn_Wd"]),
        "Wr": np.ascontiguousarray(inputs["L0_ffn_Wr"]),
        "temperature": np.ascontiguousarray(inputs["L0_ffn_temperature"]),
        "tab": np.concatenate([cos, -sin, sin], axis=1),
    }
    nc = bacc.Bacc("TRN2", target_bir_lowering=False, num_devices=1)
    args = [nc.dram_tensor(n, list(a.shape), F32, kind="ExternalInput").ap() for n, a in arrays.items()]
    args.append(nc.dram_tensor("outT", [D, N], F32, kind="ExternalOutput").ap())
    args.append(nc.dram_tensor("w_scr", [E, B], F32, kind="Internal").ap())
    args.append(nc.dram_tensor("x1_scr", [D, B], F32, kind="Internal").ap())
    build(nc, *args)
    r = run_bass_kernel_spmd(nc, [arrays], core_ids=[0])
    return np.ascontiguousarray(r.results[0]["outT"].T)[None]
```
